# Optimizing a Trainium2 kernel written in Bass

```python
import numpy as np
import jax
import jax.numpy as jnp

def _softmax(x, axis=-1):
    return jax.nn.softmax(x, axis=axis)

def _gelu(x):
    return jax.nn.gelu(x, approximate=True)

def _silu(x):
    return jax.nn.silu(x)

def _sigmoid(x):
    return jax.nn.sigmoid(x)

def _layernorm(x, axis=-1, eps=1e-05):
    m = jnp.mean(x, axis=axis, keepdims=True)
    v = jnp.var(x, axis=axis, keepdims=True)
    return (x - m) / jnp.sqrt(v + eps)

def _scatter_add(tgt, idx, src, axis=0):
    return tgt.at[idx].add(src)

def _segment_sum(src, seg, n):
    return jax.ops.segment_sum(src, seg, n)
kernel_name = 'mk_gnn_resnorm_d4_gnn_r16_f676d5'

def setup_inputs(seed: int=0):
    np.random.seed(seed)
    _w = jnp.asarray

    def _rec_inputs():
        import jax
        import jax.numpy as jnp
        _gk = jax.random.key(seed)
        x = -0.0009044 + 1 * jax.random.normal(jax.random.fold_in(_gk, 1), (6250, 16), jnp.float32)
        src = jax.random.randint(jax.random.fold_in(_gk, 2), (200000,), 0, 6250, jnp.int32)
        dst = jnp.minimum((6250 * jax.random.uniform(jax.random.fold_in(_gk, 3), (200000,)) ** 2.0).astype(jnp.int32), 99999)
        _o = jnp.argsort(dst, stable=True)
        src = src[_o]
        dst = dst[_o]
        edge_attr_16 = -3.57403e-05 + 0.999761 * jax.random.normal(jax.random.fold_in(_gk, 12), (200000, 16), jnp.float32)
        edge_weight = -0.000107899 + 1.00008 * jax.random.normal(jax.random.fold_in(_gk, 14), (200000,), jnp.float32)
        edge_weight1 = jax.random.uniform(jax.random.fold_in(_gk, 15), (200000, 1), jnp.float32, 0.0, 1)
        return (x, src, dst, edge_attr_16, edge_weight, edge_weight1)
    x, src, dst, edge_attr_16, edge_weight, edge_weight1 = _rec_inputs()

    def _L0_gnn_setup():
        import jax, jax.numpy as jnp
        import numpy as np
        N_NODES = 6250
        N_EDGES = 200000
        D_FEAT = 16
        key = jax.random.key(seed)
        k1, k2, k3, k4 = jax.random.split(key, 4)
        x = jax.random.normal(k1, (N_NODES, D_FEAT), dtype=jnp.float32)
        edge_weight = jax.random.normal(k2, (N_EDGES,), dtype=jnp.float32)
        src = jax.random.randint(k3, (N_EDGES,), 0, N_NODES, dtype=jnp.int64)
        dst = jax.random.randint(k4, (N_EDGES,), 0, N_NODES, dtype=jnp.int64)
        return {'x': x, 'edge_weight': edge_weight, 'src': src, 'dst': dst}
    _L0_gnn_all = _L0_gnn_setup()
    _L0_gnn_in = {k: v for k, v in _L0_gnn_all.items() if k in ()}
    del _L0_gnn_all

    def _L1_gnn_setup():
        import jax, jax.numpy as jnp
        import numpy as np
        N_NODES = 1875
        N_EDGES = 18750
        IN_FEATS = 16
        OUT_FEATS = 16
        EDGE_DIM = 16
        key = jax.random.key(seed)
        ks = jax.random.split(key, 8)
        feat = jax.random.normal(ks[0], (N_NODES, IN_FEATS), dtype=jnp.float32)
        efeat = jax.random.normal(ks[1], (N_EDGES, EDGE_DIM), dtype=jnp.float32)
        W_msg = jax.random.normal(ks[2], (EDGE_DIM, IN_FEATS * OUT_FEATS), dtype=jnp.float32) * 0.1
        b_msg = jnp.zeros((IN_FEATS * OUT_FEATS,), dtype=jnp.float32)
        W_attn = jax.random.normal(ks[3], (EDGE_DIM, IN_FEATS * OUT_FEATS), dtype=jnp.float32) * 0.1
        b_attn = jnp.zeros((IN_FEATS * OUT_FEATS,), dtype=jnp.float32)
        src = jax.random.randint(ks[4], (N_EDGES,), 0, N_NODES, dtype=jnp.int32)
        dst = jax.random.randint(ks[5], (N_EDGES,), 0, N_NODES, dtype=jnp.int32)
        return {'feat': feat, 'efeat': efeat, 'W_msg': W_msg, 'b_msg': b_msg, 'W_attn': W_attn, 'b_attn': b_attn, 'src': src, 'dst': dst}
    _L1_gnn_all = _L1_gnn_setup()
    _L1_gnn_in = {k: v for k, v in _L1_gnn_all.items() if k in ('W_msg', 'b_msg', 'W_attn', 'b_attn')}
    del _L1_gnn_all

    def _L2_gnn_setup():
        import jax, jax.numpy as jnp
        import numpy as np
        N_NODES = 12500
        N_RAND_EDGES = 400000
        D = 16
        key = jax.random.key(seed)
        k1, k2, k3, k4, k5, k6 = jax.random.split(key, 6)
        inputs = jax.random.normal(k1, (N_NODES, D), dtype=jnp.float32)
        src_r = jax.random.randint(k2, (N_RAND_EDGES,), 0, N_NODES, dtype=jnp.int32)
        dst_r = jax.random.randint(k3, (N_RAND_EDGES,), 0, N_NODES, dtype=jnp.int32)
        loop = jnp.arange(N_NODES, dtype=jnp.int32)
        src = jnp.concatenate([src_r, loop])
        dst = jnp.concatenate([dst_r, loop])
        E = src.shape[0]
        timestamp = jax.random.uniform(k4, (E, 1), dtype=jnp.float32)
        W = jax.random.normal(k5, (D, D), dtype=jnp.float32) * (1.0 / np.sqrt(D))
        b = jax.random.normal(k6, (D,), dtype=jnp.float32) * 0.01
        return {'inputs': inputs, 'timestamp': timestamp, 'W': W, 'b': b, 'src': src, 'dst': dst}
    _L2_gnn_all = _L2_gnn_setup()
    _L2_gnn_in = {k: v for k, v in _L2_gnn_all.items() if k in ('W', 'b')}
    del _L2_gnn_all

    def _L3_gnn_setup():
        import jax, jax.numpy as jnp
        import numpy as np
        N_NODES = 12500
        N_EDGES = 200000
        F_IN = 16
        N_CLASSES = 16

        def _gin_conv(x, src, dst, eps, wa, ba, wb, bb, n_nodes):
            agg = jax.ops.segment_sum(x[src], dst, num_segments=n_nodes)
            h = (1.0 + eps) * x + agg
            h = jax.nn.relu(h @ wa + ba) @ wb + bb
            return h
        key = jax.random.key(seed)
        ks = jax.random.split(key, 8)
        s = 1.0 / np.sqrt(F_IN)
        return {'x': jax.random.normal(ks[0], (N_NODES, F_IN), dtype=jnp.float32), 'edge_index': jax.random.randint(ks[1], (2, N_EDGES), 0, N_NODES, dtype=jnp.int32), 'eps1': jnp.zeros((), dtype=jnp.float32), 'w1a': jax.random.normal(ks[2], (F_IN, 16), dtype=jnp.float32) * s, 'b1a': jnp.zeros((16,), dtype=jnp.float32), 'w1b': jax.random.normal(ks[3], (16, 16), dtype=jnp.float32) * 0.25, 'b1b': jnp.zeros((16,), dtype=jnp.float32), 'eps2': jnp.zeros((), dtype=jnp.float32), 'w2a': jax.random.normal(ks[4], (16, N_CLASSES), dtype=jnp.float32) * 0.25, 'b2a': jnp.zeros((N_CLASSES,), dtype=jnp.float32), 'w2b': jax.random.normal(ks[5], (N_CLASSES, N_CLASSES), dtype=jnp.float32) * 0.25, 'b2b': jnp.zeros((N_CLASSES,), dtype=jnp.float32)}
    _L3_gnn_all = _L3_gnn_setup()
    _L3_gnn_in = {k: v for k, v in _L3_gnn_all.items() if k in ('eps1', 'w1a', 'b1a', 'w1b', 'b1b', 'eps2', 'w2a', 'b2a', 'w2b', 'b2b')}
    del _L3_gnn_all
    return {'x': x, 'src': src, 'dst': dst, 'edge_attr_16': edge_attr_16, 'edge_weight': edge_weight, 'edge_weight1': edge_weight1, 'L1_gnn_W_msg': _L1_gnn_in['W_msg'], 'L1_gnn_b_msg': _L1_gnn_in['b_msg'], 'L1_gnn_W_attn': _L1_gnn_in['W_attn'], 'L1_gnn_b_attn': _L1_gnn_in['b_attn'], 'L2_gnn_W': _L2_gnn_in['W'], 'L2_gnn_b': _L2_gnn_in['b'], 'L3_gnn_eps1': _L3_gnn_in['eps1'], 'L3_gnn_w1a': _L3_gnn_in['w1a'], 'L3_gnn_b1a': _L3_gnn_in['b1a'], 'L3_gnn_w1b': _L3_gnn_in['w1b'], 'L3_gnn_b1b': _L3_gnn_in['b1b'], 'L3_gnn_eps2': _L3_gnn_in['eps2'], 'L3_gnn_w2a': _L3_gnn_in['w2a'], 'L3_gnn_b2a': _L3_gnn_in['b2a'], 'L3_gnn_w2b': _L3_gnn_in['w2b'], 'L3_gnn_b2b': _L3_gnn_in['b2b']}

def reference(x, src, dst, edge_attr_16, edge_weight, edge_weight1, L1_gnn_W_msg, L1_gnn_b_msg, L1_gnn_W_attn, L1_gnn_b_attn, L2_gnn_W, L2_gnn_b, L3_gnn_eps1, L3_gnn_w1a, L3_gnn_b1a, L3_gnn_w1b, L3_gnn_b1b, L3_gnn_eps2, L3_gnn_w2a, L3_gnn_b2a, L3_gnn_w2b, L3_gnn_b2b):
    import jax
    import jax.numpy as jnp

    def _L0_gnn_ref(x, edge_weight, src, dst):
        import jax, jax.numpy as jnp
        import numpy as np
        N_NODES = 6250
        N_EDGES = 200000
        D_FEAT = 16
        m = jnp.tanh(x[src] * edge_weight[:, None])
        return jax.ops.segment_sum(m, dst, num_segments=x.shape[0])

    def _L1_gnn_ref(feat, efeat, W_msg, b_msg, W_attn, b_attn, src, dst):
        import jax, jax.numpy as jnp
        import numpy as np
        N_NODES = 1875
        N_EDGES = 18750
        IN_FEATS = 16
        OUT_FEATS = 16
        EDGE_DIM = 16
        N, in_f = feat.shape
        E = efeat.shape[0]
        w_m = (efeat @ W_msg + b_msg).reshape(E, in_f, -1)
        w_a = (efeat @ W_attn + b_attn).reshape(E, in_f, -1)
        h_src = feat[src][:, :, None]
        e1 = w_m * h_src
        e2 = w_a * h_src
        seg_max = jax.ops.segment_max(e2, dst, num_segments=N)
        ex = jnp.exp(e2 - seg_max[dst])
        denom = jax.ops.segment_sum(ex, dst, num_segments=N)
        attn = ex / denom[dst]
        ft = jax.ops.segment_sum(e1 * attn, dst, num_segments=N)
        return ft.sum(axis=1)

    def _L2_gnn_ref(inputs, timestamp, W, b, src, dst):
        import jax, jax.numpy as jnp
        import numpy as np
        N_NODES = 12500
        N_RAND_EDGES = 400000
        D = 16
        msg = inputs[src] * timestamp
        h = jax.ops.segment_max(msg, dst, num_segments=inputs.shape[0])
        return h @ W.T + b

    def _L3_gnn_ref(x, edge_index, eps1, w1a, b1a, w1b, b1b, eps2, w2a, b2a, w2b, b2b):
        import jax, jax.numpy as jnp
        import numpy as np
        N_NODES = 12500
        N_EDGES = 200000
        F_IN = 16
        N_CLASSES = 16

        def _gin_conv(x, src, dst, eps, wa, ba, wb, bb, n_nodes):
            agg = jax.ops.segment_sum(x[src], dst, num_segments=n_nodes)
            h = (1.0 + eps) * x + agg
            h = jax.nn.relu(h @ wa + ba) @ wb + bb
            return h
        src, dst = (edge_index[0], edge_index[1])
        n = x.shape[0]
        h = jax.nn.relu(_gin_conv(x, src, dst, eps1, w1a, b1a, w1b, b1b, n))
        h = _gin_conv(h, src, dst, eps2, w2a, b2a, w2b, b2b, n)
        return jax.nn.log_softmax(h, axis=1)
    edge_index = jnp.stack([src, dst])
    x = _layernorm(x + _L0_gnn_ref(x, edge_weight, src, dst), axis=-1)
    x = _layernorm(x + _L1_gnn_ref(x, edge_attr_16, L1_gnn_W_msg, L1_gnn_b_msg, L1_gnn_W_attn, L1_gnn_b_attn, src, dst), axis=-1)
    x = _layernorm(x + _L2_gnn_ref(x, edge_weight1, L2_gnn_W, L2_gnn_b, src, dst), axis=-1)
    x = _layernorm(x + _L3_gnn_ref(x, edge_index, L3_gnn_eps1, L3_gnn_w1a, L3_gnn_b1a, L3_gnn_w1b, L3_gnn_b1b, L3_gnn_eps2, L3_gnn_w2a, L3_gnn_b2a, L3_gnn_w2b, L3_gnn_b2b), axis=-1)
    return x

_drawn_inputs = setup_inputs


def setup_inputs(seed=0):
    import zlib

    import numpy as np

    out = dict(_drawn_inputs(seed))
    spreads = {'L1_gnn_b_msg': (0.0, 0.435),
     'L1_gnn_b_attn': (0.0, 0.418),
     'L3_gnn_b1a': (0.0, 0.8),
     'L3_gnn_b1b': (0.0, 0.8),
     'L3_gnn_b2a': (0.0, 0.8),
     'L3_gnn_b2b': (0.0, 0.8)}
    factors = {'edge_attr_16': 4.527, 'edge_weight1': 6.697, 'L2_gnn_b': 8.0}
    for name, (base, spread) in spreads.items():
        noise = np.random.default_rng([zlib.crc32(name.encode()), seed]).standard_normal(out[name].shape)
        drawn = base * np.exp(spread * noise) if base else spread * noise
        out[name] = jnp.asarray(drawn.astype(out[name].dtype))
    for name, factor in factors.items():
        out[name] = (out[name] * factor).astype(out[name].dtype)
    return out
```

```python
import concourse.bass as bass
from concourse import mybir
from contextlib import ExitStack

P = 128
N, E, D = 6250, 200000, 16
U = 28
G = 7
K = -(-E // (P * 2 * U)) * 2 * U
NB = -(-(N + 1) // P)
NN = P * NB
NG = K // U
AG = K // G
DD = D * D
TW = 3 * DD
BIG = 1e38
OOB = float(1 << 20)
POISON = 1e30
TINY = 1e-30
EPS = 1e-5
DC = 7
DW = DC * D
NCH = NB // DC
PB = 4
assert NB % DC == 0 and K % (2 * G) == 0 and NG >= NB and G * D == DW
CONT, BOTH, CONT_NEG, BOTH_NEG = range(4)

FP = mybir.dt.float32
I32 = mybir.dt.int32
ALU = mybir.AluOpType
ACT = mybir.ActivationFunctionType
AX = mybir.AxisListType


def gnn_program(nc, x, src, dst, ew, ew1, ef, wpad, ident, dense_w, biases, eps, out):
    es = ExitStack()

    def sb(name, shape, dt=FP):
        return es.enter_context(nc.sbuf_tensor(name, shape, dt))

    def sem(name):
        return es.enter_context(nc.semaphore(name))

    def ring(name):
        return [sem(f"{name}_{i}") for i in range(2)]

    def dram(name, shape):
        return nc.dram_tensor(name, shape, FP).ap()

    with es:
        feat = [x] + [dram(f"feat{i}", (NN, D)) for i in range(1, 5)]
        run_tab = [dram(f"run_tab{i}", (P * K, D)) for i in range(4)]
        att_tab = dram("att_tab", (NN, TW))

        idm = sb("idm", [P, P])
        ones = sb("ones", [P, P])
        edgei = sb("edgei", [P, 3], I32)
        edgef = sb("edgef", [P, 3])
        keep = sb("keep", [P, K])
        neg = sb("neg", [P, K])
        scat = sb("scat", [P, K])
        nidi = sb("nidi", [P, NG + 1], I32)
        nid = sb("nid", [P, NG + 1])
        pidx = sb("pidx", [P, NG])
        cle = sb("cle", [P, NG])
        clt = sb("clt", [P, NG])
        full = sb("full", [P, NB])
        endf = sb("endf", [P, NB])
        endi = sb("endi", [P, NB], I32)
        fcol = sb("fcol", [P, 5])
        fidx = sb("fidx", [P, 3], I32)
        diag = sb("diag", [P, 3, P])
        frow = sb("frow", [P, P])
        rows = sb("rows", [P, 4, P])

        sidx = sb("sidx", [P, 2, U], I32)
        wts = sb("wts", [P, 2, U])
        msg = sb("msg", [P, 2, U, D])
        val = sb("val", [P, 2, U, D])
        run = sb("run", [P, 2, U, D])
        mring = sb("mring", [P, 2, U])
        pring = sb("pring", [P, 2], I32)
        tailT = sb("tailT", [D, P])
        carryT = sb("carryT", [D, P])
        lead = sb("lead", [P, D])
        lead2 = sb("lead2", [P, D])

        aidx = sb("aidx", [P, 2, G], I32)
        efs = sb("efs", [P, 2, G * D])
        efT = sb("efT", [P, 2, P])
        hsrc = sb("hsrc", [P, 2, G, D])
        wsb = sb("wsb", [P, G, 2 * DD])
        aring = sb("aring", [P, 2, 2, G])
        scidx = sb("scidx", [P, 2, G], I32)
        dbuf = sb("dbuf", [P, G + 1, DD])
        bbuf = sb("bbuf", [P, 2, G + 1, 2, DD])
        amax = sb("amax", [P, 2, G, DD])
        smax = sb("smax", [P, G - 1, DD])
        st = sb("st", [P, 2, G, TW])
        stt = sb("stt", [P, 2, DD])
        tT = sb("tT", [P, 6, P])
        cT = sb("cT", [P, 6, P])
        ab = sb("ab", [P, 2, 2, P])
        zt = sb("zt", [P, TW])
        slices = amax[:].rearrange("p a g c -> p (a g c)")[:, 0:2 * K].rearrange("p (a k) -> p a k", a=2).bitcast(I32)
        dsti = slices[:, 0, :]
        dstf = bbuf[:].rearrange("p a g t c -> p (a g t c)")[:, 0:K + 2]
        flat = st[:].rearrange("p a g c -> p (a g c)")
        junk = flat[:, 0:K]
        compared = flat[:, 0:NG * P].rearrange("p (b q) -> p b q", b=NG)

        x0 = sb("x0", [P, NB, D])
        xa = sb("xa", [P, NB, D])
        xb = sb("xb", [P, NB, D])
        got = sb("got", [P, NB, D])
        nt = sb("nt", [P, NB, D])
        nu = sb("nu", [P, NB, D])
        vT = sb("vT", [P, NCH, P])
        bd = sb("bd", [P, 5, DW])
        bias = sb("bias", [P, 5, D])
        epsb = sb("epsb", [P, 2])
        st1 = sb("st1", [P, NB])
        st2 = sb("st2", [P, NB])
        st3 = sb("st3", [P, NB])
        bad = sb("bad", [P, NB])

        ps = es.enter_context(nc.psum_tensor("ps", [P, 8, 512], FP))

        s_const = sem("s_const")
        s_zero = sem("s_zero")
        s_w = sem("s_w")
        s_tab = sem("s_tab")
        s_iota = sem("s_iota")
        s_chain = sem("s_chain")
        s_loop = sem("s_loop")
        s_diag = sem("s_diag")
        s_rows = sem("s_rows")
        s_pidx = ring("s_pidx")
        s_slice = ring("s_slice")
        s_count = ring("s_count")
        s_pool = sem("s_pool")
        s_sp = sem("s_sp")
        s_idxr = sem("s_idxr")
        s_fixed = sem("s_fixed")
        s_node = [sem(f"s_node{i}") for i in range(4)]
        s_tail = sem("s_tail")
        s_turn = sem("s_turn")
        s_car = sem("s_car")
        s_back = sem("s_back")
        s_lead = sem("s_lead")
        s_att = ring("s_att")
        s_attu = sem("s_attu")
        s_feat = sem("s_feat")
        s_feats = sem("s_feats")
        s_din = sem("s_din")
        s_dtr = sem("s_dtr")
        s_dcp = sem("s_dcp")
        s_dmm = sem("s_dmm")
        s_asked = sem("s_asked")
        s_acted = sem("s_acted")
        s_out = sem("s_out")
        NARROW = ("idx", "w", "got", "mul", "act", "run", "put")
        narrow = [{k: ring(f"n{n}_{k}") for k in NARROW} for n in range(4)]
        a_idx = ring("a_idx")
        a_ef = ring("a_ef")
        a_got = ring("a_got")
        a_tr = ring("a_tr")
        a_trs = ring("a_trs")
        a_mm = ring("a_mm")
        a_read = ring("a_read")
        a_d = ring("a_d")
        a_exp = ring("a_exp")
        a_max = ring("a_max")
        a_st = ring("a_st")
        a_sc = ring("a_sc")

        HALF = NG // 2
        AHALF = AG // 2
        block = es.enter_context(nc.Block())

        @block.sync
        def _(sp):
            def narrow_pass(n):
                q = narrow[n]
                table = run_tab[n].rearrange("(p k) c -> p (k c)", p=P)

                def load(g, s):
                    sp.dma_start(sidx[:, s, :], src[:, bass.ds(g * U, U)]).then_inc(q["idx"][s], 16)
                    if n < 2:
                        sp.dma_start(wts[:, s, :], (ew, ew1)[n][:, bass.ds(g * U, U)]).then_inc(q["w"][s], 16)

                def round_(j, more):
                    for s in range(2):
                        sp.wait_ge(q["run"][s], j + 1)
                        sp.sem_inc(s_sp, 1)
                        sp.dma_start(table[:, bass.ds((2 * j + s) * (U * D), U * D)],
                                     run[:, s].rearrange("p u c -> p (u c)")).then_inc(q["put"][s], 16)
                        if more:
                            load(2 * j + 2 + s, s)

                for s in range(2):
                    load(s, s)
                with sp.Fori(0, HALF - 1) as j:
                    round_(j, True)
                round_(HALF - 1, False)

            def put_feat(i, tile):
                sp.wait_ge(s_feat, i)
                sp.dma_start(feat[i].rearrange("(p b) c -> p (b c)", p=P),
                             tile[:].rearrange("p b c -> p (b c)")).then_inc(s_feats, 16)

            def attention():
                def load(g, s):
                    sp.dma_start(aidx[:, s, :], src[:, bass.ds(g * G, G)]).then_inc(a_idx[s], 16)
                    sp.dma_start(efs[:, s, :], ef[:, bass.ds(g * (G * D), G * D)]).then_inc(a_ef[s], 16)

                for s in range(2):
                    load(s, s)
                with sp.Fori(0, AHALF - 1) as j:
                    for s in range(2):
                        sp.wait_ge(a_tr[s], j + 1)
                        sp.sem_inc(s_sp, 1)
                        sp.wait_ge(a_got[s], (j + 1) * (16 * G))
                        sp.sem_inc(s_sp, 1)
                        load(2 * j + 2 + s, s)
                states = att_tab.rearrange("(p b) c -> p b c", p=P)
                sp.wait_ge(s_fixed, 16 * 4)
                for c in range(NCH):
                    if c >= 2:
                        sp.wait_ge(s_attu, c - 1)
                    sp.dma_start(bbuf[:, c % 2, 0:DC].rearrange("p b t c -> p b (t c)"),
                                 states[:, c * DC:(c + 1) * DC, 0:2 * DD]).then_inc(s_att[c % 2], 16)

            narrow_pass(0)
            put_feat(1, xa)
            attention()
            put_feat(2, xb)
            narrow_pass(1)
            put_feat(3, xa)
            narrow_pass(2)
            put_feat(4, xb)
            narrow_pass(3)
            sp.wait_ge(s_feat, 5)
            sp.dma_start(out.rearrange("(p b) c -> p (b c)", p=P),
                         nt[:].rearrange("p b c -> p (b c)")).then_inc(s_out, 16)
            sp.wait_ge(s_out, 16)

        @block.gpsimd
        def _(pool):
            def rows_at(ap):
                return bass.IndirectOffsetOnAxis(ap=ap, axis=0)

            def gather(dest, table, idx):
                return pool.indirect_dma_start(dest, None, table, rows_at(idx))

            def scatter(table, idx, source, **kw):
                return pool.indirect_dma_start(table, rows_at(idx), source, None, **kw)

            def narrow_pass(n, table):
                q = narrow[n]
                used = q["mul"] if n < 2 else q["run"]
                with pool.Fori(0, HALF) as j:
                    for s in range(2):
                        pool.wait_ge(q["idx"][s], 16 * (j + 1))
                        pool.wait_ge(used[s], j)
                        pool.sem_inc(s_pool, 1)
                        for u in range(U):
                            gather(msg[:, s, u, :], table, sidx[:, s, u:u + 1]).then_inc(q["got"][s], 16)
                        if n == 0:
                            pool.wait_ge(s_pidx[s], j + 1)
                            pool.sem_inc(s_pool, 1)
                            gather(slices[:, s, :], dst, pring[:, s:s + 1]).then_inc(s_slice[s], 16)
                if n == 0:
                    pool.wait_ge(s_idxr, 1)
                for s in range(2):
                    pool.wait_ge(q["put"][s], 16 * HALF)
                fixes = 2 * n if n == 0 else 2 * n + 2
                gather(lead[:], run_tab[n], fidx[:, 0:1]).then_inc(s_fixed, 16)
                pool.wait_ge(s_lead, fixes // 2 + 1)
                scatter(run_tab[n], fidx[:, 0:1], lead2[:]).then_inc(s_fixed, 16)
                pool.wait_ge(s_fixed, 16 * (fixes + 2))
                for b in range(NB):
                    gather(got[:, b, :], run_tab[n], endi[:, b:b + 1]).then_inc(s_node[n], 16)

            def attention():
                def group(j, s, store):
                    pool.wait_ge(a_idx[s], 16 * (j + 1))
                    pool.wait_ge(a_read[s], j)
                    pool.sem_inc(s_pool, 1)
                    for k in range(G):
                        gather(hsrc[:, s, k, :], feat[1], aidx[:, s, k:k + 1]).then_inc(a_got[s], 16)
                    if store:
                        put(j, s)

                def put(j, s):
                    pool.wait_ge(a_st[s], j)
                    pool.sem_inc(s_pool, 1)
                    for k in range(G):
                        scatter(att_tab, scidx[:, s, k:k + 1], st[:, s, k, :],
                                bounds_check=NN - 1, oob_is_err=False).then_inc(a_sc[s], 16)

                pool.wait_ge(s_tab, 16)
                for s in range(2):
                    group(0, s, False)
                with pool.Fori(1, AHALF) as j:
                    for s in range(2):
                        group(j, s, True)
                for s in range(2):
                    put(AHALF, s)
                for s in range(2):
                    pool.wait_ge(a_sc[s], 16 * G * AHALF)
                pool.wait_ge(s_tail, 2)
                gather(st[:, 0, 0, :], att_tab, fidx[:, 1:2]).then_inc(s_fixed, 16)
                pool.wait_ge(s_lead, 2)
                scatter(att_tab, fidx[:, 2:3], st[:, 0, 1, :],
                        bounds_check=NN - 1, oob_is_err=False).then_inc(s_fixed, 16)

            pool.memset(bd[:], 0.0).then_inc(s_zero, 1)
            pool.memset(wsb[:], 0.0).then_inc(s_zero, 1)
            pool.memset(zt[:], 0.0).then_inc(s_zero, 1)
            pool.memset(efT[:], 1.0).then_inc(s_zero, 1)
            pool.memset(ones[:], 1.0).then_inc(s_zero, 1)
            pool.iota(nidi[:, 0:NG], [[1, NG]], base=0, channel_multiplier=NB).then_inc(s_iota, 1)
            pool.iota(nidi[:, NG:NG + 1], [[0, 1]], base=-1, channel_multiplier=K).then_inc(s_iota, 1)
            narrow_pass(0, feat[0])
            pool.wait_ge(s_feats, 16)
            attention()
            for n in range(1, 4):
                pool.wait_ge(s_feats, 16 * (n + 1))
                narrow_pass(n, feat[n + 1])

        @block.scalar
        def _(act):
            acted = [0]

            def asked(dest, source, func):
                acted[0] += 1
                act.wait_ge(s_asked, acted[0])
                nc.scalar.activation(dest, source, func).then_inc(s_acted, 1)

            def dense(i):
                act.wait_ge(s_dtr, i + 1)
                nc.scalar.activation(vT[0:DW, 0:PB, :], ps[0:DW, 0, 0:PB * P].rearrange("p (c q) -> p c q", q=P), ACT.Copy)
                nc.scalar.activation(vT[0:DW, PB:NCH, :], ps[0:DW, 1, 0:(NCH - PB) * P].rearrange("p (c q) -> p c q", q=P),
                                     ACT.Copy).then_inc(s_dcp, 1)

            act.dma_start(dsti, dst[1:P + 1, :]).then_inc(s_const, 16)
            for c, (r, k) in enumerate(((0, K - 1), (0, 0), (2, 0))):
                act.dma_start(edgei[:, c:c + 1], dst[r:r + P, k:k + 1], allow_slow_non_contiguous=True).then_inc(s_const, 16)
            act.dma_start(idm[:], ident).then_inc(s_const, 16)
            act.dma_start(x0[:].rearrange("p b c -> p (b c)"), x.rearrange("(p b) c -> p (b c)", p=P)).then_inc(s_const, 16)
            for i in range(2):
                act.dma_start(epsb[:, i:i + 1], eps[i:i + 1].partition_broadcast(P)).then_inc(s_const, 16)
            for i in range(5):
                act.dma_start(bias[:, i, :], biases[i].partition_broadcast(P)).then_inc(s_const, 16)
            act.wait_ge(s_zero, 3)
            for i in range(5):
                for c in range(DC):
                    act.dma_start(bd[c * D:(c + 1) * D, i, c * D:(c + 1) * D], dense_w[i]).then_inc(s_w, 16)
            for c in range(G):
                act.dma_start(wsb[c * D:(c + 1) * D, c, :], wpad[0:D, :]).then_inc(s_w, 16)
                act.dma_start(wsb[DW:DW + 1, c, :], wpad[D:D + 1, :]).then_inc(s_w, 16)
            act.dma_start(att_tab.rearrange("(p b) c -> p b c", p=P),
                          zt[:].unsqueeze(1).to_broadcast([P, NB, TW])).then_inc(s_tab, 16)
            q = narrow[0]
            with act.Fori(0, HALF) as j:
                for s in range(2):
                    act.wait_ge(q["mul"][s], j + 1)
                    nc.scalar.activation(val[:, s], val[:, s], ACT.Tanh).then_inc(q["act"][s], 1)
            asked(st3[:], st2[:], ACT.Sqrt)

            act.wait_ge(s_zero, 4)

            def turn_copy(j, s):
                act.wait_ge(a_tr[s], j + 1)
                nc.scalar.activation(efT[0:DW, s, :], ps[0:DW, G, 0:P], ACT.Copy).then_inc(a_trs[s], 1)

            def group(j, s, more, old):
                if more:
                    turn_copy(j + s, 1 - s)
                act.wait_ge(a_d[s], j + 1)
                nc.scalar.activation(bbuf[:, s, :, 0, :], dbuf[:], ACT.Exp).then_inc(a_exp[s], 1)
                if old:
                    act.wait_ge(a_sc[s], j * (16 * G))
                nc.scalar.activation(st[:, s, :, 2 * DD:TW], amax[:, s], ACT.Copy).then_inc(a_max[s], 1)

            turn_copy(0, 0)
            for s in range(2):
                group(0, s, True, False)
            with act.Fori(1, AHALF - 1) as j:
                for s in range(2):
                    group(j, s, True, True)
            group(AHALF - 1, 0, True, True)
            group(AHALF - 1, 1, False, True)
            asked(ab[:], ab[:], ACT.Exp)
            asked(bbuf[:, 0, 0], bbuf[:, 0, 0], ACT.Exp)
            asked(st3[:], st2[:], ACT.Sqrt)
            dense(0)
            asked(st3[:], st2[:], ACT.Sqrt)
            for i in range(1, 5):
                dense(i)
            asked(nu[:], nt[:], ACT.Exp)
            asked(st2[:], st1[:], ACT.Ln)
            asked(st3[:], st2[:], ACT.Sqrt)

        @block.tensor
        def _(pe):
            def carry(i, tail):
                pe.wait_ge(s_tail, 1 + i)
                m = tail.shape[1]
                for c in range(-(-m // P)):
                    w = min(P, m - c * P)
                    last = nc.tensor.transpose(ps[0:w, c // PB, (c % PB) * P:(c % PB + 1) * P], tail[:, c * P:c * P + w], idm[:])
                last.then_inc(s_turn, 1)
                pe.wait_ge(s_car, 1 + i)
                for c in range(-(-m // P)):
                    w = min(P, m - c * P)
                    source = cT[:, c, :] if m > P else carryT[:]
                    last = nc.tensor.transpose(ps[:, 2 + c // PB, (c % PB) * P:(c % PB) * P + w], source, idm[0:w, 0:w])
                last.then_inc(s_back, 1)

            def dense(i, w, v):
                pe.wait_ge(s_din, i + 1)
                for c in range(NCH):
                    last = nc.tensor.transpose(ps[0:DW, c // PB, (c % PB) * P:(c % PB + 1) * P],
                                               v[:, c * DC:(c + 1) * DC, :].rearrange("p b c -> p (b c)"), idm[:])
                last.then_inc(s_dtr, 1)
                pe.wait_ge(s_dcp, i + 1)
                for c in range(NCH):
                    last = nc.tensor.matmul(ps[:, 2 + c // PB, (c % PB) * DW:(c % PB + 1) * DW], vT[0:DW, c, :], bd[0:DW, w, :],
                                            start=True, stop=True)
                last.then_inc(s_dmm, 1)

            pe.wait_ge(s_zero, 5)
            pe.wait_ge(s_diag, 1)
            nc.tensor.matmul(ps[:, 0, 0:3 * P], ones[:], diag[:].rearrange("p a q -> p (a q)"), start=True, stop=True).then_inc(s_rows, 1)
            tail = run[:, 1, U - 1, :]
            carry(0, tail)

            pe.wait_ge(s_w, 16 * (5 * DC + 2 * G))

            def turn(j, s):
                pe.wait_ge(a_ef[s], 16 * (j + 1))
                nc.tensor.transpose(ps[0:DW, G, 0:P], efs[:, s, :], idm[:]).then_inc(a_tr[s], 1)

            def group(j, s, more, old):
                pe.wait_ge(a_trs[s], j + 1)
                if more:
                    turn(j + s, 1 - s)
                if old:
                    pe.wait_ge(a_read[1 - s], j + s)
                for k in range(G):
                    last = nc.tensor.matmul(ps[:, k, :], efT[0:DW + 1, s, :], wsb[0:DW + 1, k, :], start=True, stop=True)
                last.then_inc(a_mm[s], 1)

            pe.wait_ge(s_feat, 1)
            turn(0, 0)
            group(0, 0, True, False)
            group(0, 1, True, True)
            with pe.Fori(1, AHALF - 1) as j:
                for s in range(2):
                    group(j, s, True, True)
            group(AHALF - 1, 0, True, True)
            group(AHALF - 1, 1, False, True)
            carry(1, st[:, 1, G - 1, :])
            carry(2, tail)
            dense(0, 0, nt)
            carry(3, tail)
            dense(1, 1, nt)
            dense(2, 2, nt)
            carry(4, tail)
            dense(3, 3, nt)
            dense(4, 4, nt)

        @block.vector
        def _(dve):
            v = nc.vector
            chained = [0]
            looped = [0]

            def link(ins):
                chained[0] += 1
                ins.then_inc(s_chain, 1)
                dve.wait_ge(s_chain, chained[0])

            def loop_start():
                looped[0] = 0
                dve.sem_clear(s_loop)

            def hold(ins):
                looped[0] += 1
                ins.then_inc(s_loop, 1)
                dve.wait_ge(s_loop, looped[0])

            def wide(ap):
                return ap.unsqueeze(2).to_broadcast([P, ap.shape[1], D])

            def everywhere(row):
                return row.unsqueeze(1).to_broadcast([P, NB, D])

            def tt(dest, a, b, op):
                return v.tensor_tensor(dest, a, b, op)

            asks = [0]

            def ask(ins):
                asks[0] += 1
                ins.then_inc(s_asked, 1)
                dve.wait_ge(s_acted, asks[0])

            dve.wait_ge(s_const, 16 * 13)
            dve.wait_ge(s_iota, 2)
            link(v.tensor_copy(dstf[:, 1:K + 1], dsti))
            link(v.tensor_copy(edgef[:], edgei[:]))
            link(v.tensor_copy(dstf[:, 0:1], edgef[:, 0:1]))
            link(v.tensor_copy(dstf[:, K + 1:K + 2], edgef[:, 2:3]))
            link(v.tensor_copy(nid[:], nidi[:]))
            first = dstf[:, 1:2]
            link(tt(fcol[:, 0:1], first, dstf[:, 0:1], ALU.is_equal))
            link(tt(fcol[:, 1:2], edgef[:, 0:1], edgef[:, 1:2], ALU.is_equal))
            link(tt(fcol[:, 1:2], fcol[:, 0:1], fcol[:, 1:2], ALU.mult))
            link(v.tensor_scalar(diag[:, 0, :], idm[:], first, None, ALU.mult))
            link(v.tensor_scalar(diag[:, 1, :], idm[:], fcol[:, 0:1], None, ALU.mult))
            v.tensor_scalar(diag[:, 2, :], idm[:], fcol[:, 1:2], None, ALU.mult).then_inc(s_diag, 1)
            link(tt(keep[:], dstf[:, 1:K + 1], dstf[:, 0:K], ALU.is_equal))
            link(v.memset(keep[:, 0:1], 0.0))
            link(v.tensor_scalar(neg[:], keep[:], 1.0, BIG, ALU.subtract, ALU.mult))
            link(tt(scat[:], dstf[:, 1:K + 1], dstf[:, 2:K + 2], ALU.is_equal))
            link(v.scalar_tensor_tensor(scat[:], scat[:], OOB, dstf[:, 1:K + 1], ALU.mult, ALU.add))
            link(v.tensor_scalar(junk, dstf[:, 1:K + 1], first, 0.0, ALU.is_equal, ALU.add, accum_out=fcol[:, 2:3]))
            link(tt(fidx[:, 0:1], fcol[:, 2:3], nid[:, NG:NG + 1], ALU.add))
            link(v.tensor_copy(fidx[:, 1:2], first))
            link(tt(fcol[:, 3:4], first, dstf[:, K + 1:K + 2], ALU.is_equal))
            link(v.tensor_scalar(fcol[:, 3:4], fcol[:, 3:4], -1.0, 1.0, ALU.mult, ALU.add))
            link(tt(fcol[:, 3:4], fcol[:, 3:4], fcol[:, 0:1], ALU.mult))
            link(v.tensor_scalar(fcol[:, 3:4], fcol[:, 3:4], -OOB, OOB, ALU.mult, ALU.add))
            link(tt(fidx[:, 2:3], fcol[:, 3:4], first, ALU.add))
            dve.wait_ge(s_rows, 1)
            link(v.tensor_copy(frow[:], ps[:, 0, 0:P]))
            link(v.tensor_copy(rows[:, 0:2, :], ps[:, 0, P:3 * P].rearrange("p (a q) -> p a q", q=P)))
            link(v.tensor_scalar(rows[:, 2:4, :], rows[:, 0:2, :], 1.0, BIG, ALU.subtract, ALU.mult))
            link(tt(compared, frow[:].unsqueeze(1).to_broadcast([P, NG, P]),
                    nid[:, 0:NG].unsqueeze(2).to_broadcast([P, NG, P]), ALU.is_le))
            link(v.tensor_reduce(pidx[:], compared, AX.X, ALU.add))
            link(v.tensor_scalar(pidx[:], pidx[:], 1.0, None, ALU.max))

            def narrow_pass(n):
                q = narrow[n]
                most = n == 1
                mask = neg if most else keep

                def next_slice(g, s):
                    v.tensor_copy(pring[:, s:s + 1], pidx[:, bass.ds(g, 1)]).then_inc(s_pidx[s], 1)

                def round_(j, more):
                    loop_start()
                    for s in range(2):
                        g = 2 * j + s
                        hold(v.tensor_copy(mring[:, s, :], mask[:, bass.ds(g * U, U)]))
                        dve.wait_ge(q["got"][s], (j + 1) * (16 * U))
                        values = msg
                        if n < 2:
                            dve.wait_ge(q["w"][s], 16 * (j + 1))
                            tt(val[:, s], msg[:, s], wts[:, s, :].unsqueeze(2).to_broadcast([P, U, D]),
                               ALU.mult).then_inc(q["mul"][s], 1)
                            values = val
                            dve.wait_ge(q["act"][s] if n == 0 else q["mul"][s], j + 1)
                        dve.wait_ge(q["put"][s], 16 * j)
                        for c in range(D):
                            last = v.tensor_tensor_scan(run[:, s, :, c], mring[:, s, :], values[:, s, :, c], run[:, 1 - s, U - 1, c:c + 1],
                                                        ALU.add if most else ALU.mult, ALU.max if most else ALU.add)
                        last.then_inc(q["run"][s], 1)
                        dve.wait_ge(q["run"][s], j + 1)
                        if n == 0:
                            dve.wait_ge(s_slice[s], 16 * (j + 1))
                            node = nid[:, bass.ds(g, 1)]
                            hold(v.tensor_scalar(junk, slices[:, s, :], node, 0.0, ALU.is_le, ALU.add,
                                                 accum_out=cle[:, bass.ds(g, 1)]))
                            hold(v.tensor_scalar(junk, slices[:, s, :], node, 0.0, ALU.is_lt, ALU.add,
                                                 accum_out=clt[:, bass.ds(g, 1)]))
                            if more:
                                next_slice(g + 2, s)

                link(v.memset(run[:, 1, U - 1, :], 0.0))
                if n == 0:
                    for s in range(2):
                        next_slice(s, s)
                    with dve.Fori(0, HALF - 1) as j:
                        round_(j, True)
                    round_(HALF - 1, False)
                    link(v.tensor_scalar(endf[:], pidx[:, 0:NB], -1.0, float(K), ALU.add, ALU.mult))
                    link(tt(endf[:], endf[:], cle[:, 0:NB], ALU.add))
                    link(v.tensor_scalar(endf[:], endf[:], -1.0, 0.0, ALU.add, ALU.max))
                    link(tt(full[:], clt[:, 0:NB], cle[:, 0:NB], ALU.is_lt))
                    link(v.tensor_scalar(st1[:], nid[:, 0:NB], float(N), None, ALU.is_ge))
                    link(tt(full[:], full[:], st1[:], ALU.max))
                    v.tensor_copy(endi[:], endf[:]).then_inc(s_idxr, 1)
                else:
                    with dve.Fori(0, HALF) as j:
                        round_(j, False)
                i = 0 if n == 0 else n + 1
                v.memset(tailT[:, 0:1], -BIG if most else 0.0).then_inc(s_tail, 1)
                dve.wait_ge(s_turn, i + 1)
                link(tt(tailT[:, 1:P], ps[0:D, 0, 0:P - 1], rows[0:D, CONT_NEG if most else CONT, 1:P], ALU.add if most else ALU.mult))
                v.tensor_tensor_scan(carryT[:], rows[0:D, BOTH_NEG if most else BOTH, :], tailT[:], 0.0,
                                     ALU.add if most else ALU.mult, ALU.max if most else ALU.add).then_inc(s_car, 1)
                dve.wait_ge(s_back, i + 1)
                dve.wait_ge(s_fixed, 16 * (2 * i + 1))
                tt(lead2[:], lead[:], ps[:, 2, 0:D], ALU.max if most else ALU.add).then_inc(s_lead, 1)
                dve.wait_ge(s_node[n], 16 * NB)

            def layer_norm(dest, source):
                link(v.tensor_reduce(st1[:], source[:], AX.X, ALU.add))
                link(v.tensor_scalar(st1[:], st1[:], 1.0 / D, None, ALU.mult))
                link(tt(nt[:], source[:], wide(st1[:]), ALU.subtract))
                link(tt(nu[:], nt[:], nt[:], ALU.mult))
                link(v.tensor_reduce(st2[:], nu[:], AX.X, ALU.add))
                ask(v.tensor_scalar(st2[:], st2[:], 1.0 / D, EPS, ALU.mult, ALU.add))
                link(v.reciprocal(st3[:], st3[:]))
                return tt(dest[:], nt[:], wide(st3[:]), ALU.mult)

            def attention():
                link(v.memset(amax[:, 1, G - 1, :], 0.0))
                link(v.memset(st[:, 1, G - 1, 0:2 * DD], 0.0))

                def front(j, s, old):
                    dve.wait_ge(a_got[s], (j + 1) * (16 * G))
                    dve.wait_ge(a_mm[s], j + 1)
                    if old or s:
                        dve.wait_ge(a_exp[1 - s], j + s)
                    if old:
                        dve.wait_ge(a_max[s], j)
                    h = hsrc[:, s].unsqueeze(3).to_broadcast([P, G, D, D])
                    for b, dest in ((0, dbuf[:, 0:G, :]), (1, bbuf[:, s, 0:G, 1, :])):
                        last = tt(dest.rearrange("p g (i o) -> p g i o", o=D),
                                  ps[:, 0:G, b * DD:(b + 1) * DD].rearrange("p g (i o) -> p g i o", o=D), h, ALU.mult)
                    last.then_inc(a_read[s], 1)
                    g = 2 * j + s
                    v.tensor_copy(aring[:, s, 0, :], neg[:, bass.ds(g * G, G)])
                    hold(v.tensor_copy(aring[:, s, 1, :], keep[:, bass.ds(g * G, G)]))
                    before = amax[:, 1 - s, G - 1, :]
                    for k in range(G):
                        hold(v.scalar_tensor_tensor(amax[:, s, k, :], before if k == 0 else amax[:, s, k - 1, :],
                                                    aring[:, s, 0, k:k + 1], dbuf[:, k, :], ALU.add, ALU.max))
                    for k in range(G - 2, -1, -1):
                        hold(v.scalar_tensor_tensor(smax[:, k, :], amax[:, s, G - 1, :] if k == G - 2 else smax[:, k + 1, :],
                                                    aring[:, s, 0, k + 1:k + 2], amax[:, s, k, :], ALU.add, ALU.max))
                    tt(dbuf[:, 0:G - 1, :], dbuf[:, 0:G - 1, :], smax[:], ALU.subtract)
                    tt(dbuf[:, G - 1, :], dbuf[:, G - 1, :], amax[:, s, G - 1, :], ALU.subtract)
                    v.scalar_tensor_tensor(dbuf[:, G, :], before, aring[:, s, 0, 0:1], smax[:, 0, :], ALU.add, ALU.subtract).then_inc(a_d[s], 1)

                def back(j, s, old):
                    g = 2 * j + s
                    dve.wait_ge(a_exp[s], j + 1)
                    b = bbuf[:, s]
                    hold(tt(b[:, 0:G, 1, :], b[:, 0:G, 1, :], b[:, 0:G, 0, :], ALU.mult))
                    hold(tt(stt[:], st[:, 1 - s, G - 1, 0:2 * DD].rearrange("p (t c) -> p t c", t=2),
                            b[:, G, 0, :].unsqueeze(1).to_broadcast([P, 2, DD]), ALU.mult))
                    if old:
                        dve.wait_ge(a_sc[s], j * (16 * G))
                    dve.wait_ge(a_max[s], j + 1)
                    v.tensor_copy(scidx[:, s, :], scat[:, bass.ds(g * G, G)])
                    hold(tt(st[:, s, 0, 0:2 * DD].rearrange("p (t c) -> p t c", t=2), stt[:], b[:, 0, :, :], ALU.add))
                    for k in range(1, G):
                        last = v.scalar_tensor_tensor(st[:, s, k, 0:2 * DD], st[:, s, k - 1, 0:2 * DD], aring[:, s, 1, k:k + 1],
                                                      b[:, k, :, :].rearrange("p t c -> p (t c)"), ALU.mult, ALU.add)
                        if k < G - 1:
                            hold(last)
                    last.then_inc(a_st[s], 1)
                    dve.wait_ge(a_st[s], j + 1)

                loop_start()
                front(0, 0, False)
                front(0, 1, False)
                back(0, 0, False)
                with dve.Fori(1, AHALF) as j:
                    loop_start()
                    front(j, 0, True)
                    back(j - 1, 1, True)
                    front(j, 1, True)
                    back(j, 0, True)
                loop_start()
                back(AHALF - 1, 1, True)

                for half in range(2):
                    link(v.memset(tT[:, 4 + half, 0:1], -BIG))
                v.memset(tT[:, 0:4, 0:1], 0.0).then_inc(s_tail, 1)
                dve.wait_ge(s_turn, 2)
                link(v.tensor_copy(tT[:, 0:4, 1:P], ps[:, 0, :].rearrange("p (c q) -> p c q", q=P)[:, :, 0:P - 1]))
                for half in range(2):
                    m, c = tT[:, 4 + half, :], cT[:, 4 + half, :]
                    link(tt(m[:, 1:P], ps[:, 1, half * P:half * P + P - 1], rows[:, CONT_NEG, 1:P], ALU.add))
                    link(v.tensor_tensor_scan(c, rows[:, BOTH_NEG, :], m, 0.0, ALU.add, ALU.max))
                    link(v.memset(ab[:, half, 0, 0:1], 0.0))
                    link(tt(ab[:, half, 0, 1:P], rows[:, BOTH_NEG, 1:P], c[:, 0:P - 1], ALU.add))
                    link(tt(ab[:, half, 0, 1:P], ab[:, half, 0, 1:P], c[:, 1:P], ALU.subtract))
                    last = tt(ab[:, half, 1, :], m, c, ALU.subtract)
                    if half == 0:
                        link(last)
                ask(last)
                for t in range(4):
                    link(tt(tT[:, t, :], tT[:, t, :], ab[:, t % 2, 1, :], ALU.mult))
                    last = v.tensor_tensor_scan(cT[:, t, :], ab[:, t % 2, 0, :], tT[:, t, :], 0.0, ALU.mult, ALU.add)
                last.then_inc(s_car, 1)
                dve.wait_ge(s_back, 2)
                dve.wait_ge(s_fixed, 16 * 3)
                mine, done, w = st[:, 0, 0, :], st[:, 0, 1, :], bbuf[:, 0, 0]
                theirs = stt[:].rearrange("p t c -> p (t c)")
                link(tt(done[:, 2 * DD:TW], mine[:, 2 * DD:TW], ps[:, 3, 0:DD], ALU.max))
                link(tt(w[:, 0, :], mine[:, 2 * DD:TW], done[:, 2 * DD:TW], ALU.subtract))
                ask(tt(w[:, 1, :], ps[:, 3, 0:DD], done[:, 2 * DD:TW], ALU.subtract))
                for t in range(2):
                    part = slice(t * DD, (t + 1) * DD)
                    link(tt(theirs[:, part], ps[:, 2, part], w[:, 1, :], ALU.mult))
                    link(tt(done[:, part], mine[:, part], w[:, 0, :], ALU.mult))
                link(tt(done[:, 0:2 * DD], done[:, 0:2 * DD], theirs, ALU.add))
                link(v.memset(nt[:, 0:1, :], 0.0))
                v.memset(nt[:, 0:1, :], 0.0).then_inc(s_lead, 1)

                for c in range(NCH):
                    dve.wait_ge(s_att[c % 2], 16 * (c // 2 + 1))
                    b = bbuf[:, c % 2, 0:DC]
                    link(v.tensor_scalar(b[:, :, 0, :], b[:, :, 0, :], TINY, None, ALU.max))
                    link(v.reciprocal(b[:, :, 0, :], b[:, :, 0, :]))
                    tt(dbuf[:, 0:DC, :], b[:, :, 1, :], b[:, :, 0, :], ALU.mult).then_inc(s_attu, 1)
                    dve.wait_ge(s_attu, c + 1)
                    link(v.tensor_reduce(got[:, c * DC:(c + 1) * DC, :], dbuf[:, 0:DC, :].rearrange("p b (i o) -> p b o i", o=D), AX.X, ALU.add))

            products = [0]

            def dense(dest, ins, b, relu):
                ins.then_inc(s_din, 1)
                products[0] += 1
                dve.wait_ge(s_dmm, products[0])
                for half, (lo, hi) in enumerate(((0, PB * DC), (PB * DC, NB))):
                    link(tt(dest[:, lo:hi, :], ps[:, 2 + half, 0:(hi - lo) * D].rearrange("p (b c) -> p b c", c=D),
                            bias[:, b, :].unsqueeze(1).to_broadcast([P, hi - lo, D]), ALU.add))
                if relu:
                    link(v.tensor_scalar(dest[:], dest[:], 0.0, None, ALU.max))

            narrow_pass(0)
            link(tt(got[:], got[:], wide(full[:]), ALU.mult))
            link(tt(got[:], got[:], x0[:], ALU.add))
            layer_norm(xa, got).then_inc(s_feat, 1)
            attention()
            link(tt(got[:], got[:], xa[:], ALU.add))
            layer_norm(xb, got).then_inc(s_feat, 1)
            dve.wait_ge(s_feat, 2)
            narrow_pass(1)
            dense(got, tt(nt[:], got[:], wide(full[:]), ALU.mult), 0, False)
            link(tt(got[:], got[:], xb[:], ALU.add))
            link(layer_norm(xa, got))
            link(v.tensor_scalar(bad[:], full[:], -POISON, POISON, ALU.mult, ALU.add))
            link(tt(xa[:], xa[:], wide(full[:]), ALU.mult))
            tt(xa[:], xa[:], wide(bad[:]), ALU.add).then_inc(s_feat, 1)
            dve.wait_ge(s_feat, 3)
            for i, (own, dest) in enumerate(((xa, xb), (xb, got))):
                narrow_pass(2 + i)
                link(tt(nu[:], got[:], wide(full[:]), ALU.mult))
                link(tt(nt[:], nu[:], own[:], ALU.add))
                link(v.tensor_scalar(bad[:], nt[:, :, 0], POISON * 0.5, None, ALU.is_gt))
                link(v.tensor_scalar(st1[:], bad[:], -1.0, 1.0, ALU.mult, ALU.add))
                link(v.scalar_tensor_tensor(nt[:], own[:], epsb[:, i:i + 1], nt[:], ALU.mult, ALU.add))
                dense(got, tt(nt[:], nt[:], wide(st1[:]), ALU.mult), 1 + 2 * i, True)
                dense(dest, v.tensor_copy(nt[:], got[:]), 2 + 2 * i, i == 0)
                if i == 0:
                    link(tt(dest[:], dest[:], wide(st1[:]), ALU.mult))
                    link(v.tensor_scalar(st2[:], bad[:], POISON, None, ALU.mult))
                    tt(dest[:], dest[:], wide(st2[:]), ALU.add).then_inc(s_feat, 1)
                    dve.wait_ge(s_feat, 4)
            link(v.tensor_reduce(st1[:], got[:], AX.X, ALU.max))
            ask(tt(nt[:], got[:], wide(st1[:]), ALU.subtract))
            ask(v.tensor_reduce(st1[:], nu[:], AX.X, ALU.add))
            link(tt(nt[:], nt[:], wide(st2[:]), ALU.subtract))
            link(v.tensor_scalar(st1[:], bad[:], -1.0, 1.0, ALU.mult, ALU.add))
            link(tt(xa[:], xa[:], wide(st1[:]), ALU.mult))
            link(tt(got[:], nt[:], xa[:], ALU.add))
            link(layer_norm(got, got))
            link(v.tensor_scalar(bad[:], bad[:], BIG, BIG, ALU.mult, ALU.mult))
            link(tt(bad[:], bad[:], bad[:], ALU.subtract))
            tt(nt[:], got[:], wide(bad[:]), ALU.add).then_inc(s_feat, 1)


def kernel(x, src, dst, edge_attr_16, edge_weight, edge_weight1, L1_gnn_W_msg, L1_gnn_b_msg, L1_gnn_W_attn,
           L1_gnn_b_attn, L2_gnn_W, L2_gnn_b, L3_gnn_eps1, L3_gnn_w1a, L3_gnn_b1a, L3_gnn_w1b, L3_gnn_b1b,
           L3_gnn_eps2, L3_gnn_w2a, L3_gnn_b2a, L3_gnn_w2b, L3_gnn_b2b):
    import numpy as np
    import concourse.bacc as bacc
    from concourse.bass_utils import run_bass_kernel_spmd as run

    def padded(a, rows, fill=0):
        a = np.asarray(a)
        return np.concatenate([a, np.full((rows - a.shape[0],) + a.shape[1:], fill, a.dtype)])

    d = np.asarray(dst)
    arrays = {
        "x": padded(x, NN),
        "src": padded(src, P * K).reshape(P, K),
        "dst": np.concatenate([np.full((1, K), -1, d.dtype), padded(d, P * K, N).reshape(P, K), np.full((1, K), N + 1, d.dtype)]),
        "ew": padded(edge_weight, P * K).reshape(P, K),
        "ew1": padded(edge_weight1, P * K).reshape(P, K),
        "ef": padded(edge_attr_16, P * K).reshape(P, K * D),
        "wpad": np.concatenate([
            np.concatenate([np.asarray(L1_gnn_W_attn), np.asarray(L1_gnn_W_msg)], 1),
            np.concatenate([np.asarray(L1_gnn_b_attn), np.asarray(L1_gnn_b_msg)])[None]]),
        "ident": np.eye(P, dtype=np.float32),
        "dense_w": np.stack([np.asarray(L2_gnn_W).T] + [np.asarray(w) for w in (L3_gnn_w1a, L3_gnn_w1b, L3_gnn_w2a, L3_gnn_w2b)]),
        "biases": np.stack([np.asarray(b) for b in (L2_gnn_b, L3_gnn_b1a, L3_gnn_b1b, L3_gnn_b2a, L3_gnn_b2b)]),
        "eps": np.stack([np.asarray(L3_gnn_eps1), np.asarray(L3_gnn_eps2)]),
    }
    arrays = {k: np.ascontiguousarray(v) for k, v in arrays.items()}
    nc = bacc.Bacc("TRN2", target_bir_lowering=False, num_devices=1)
    args = [nc.dram_tensor(f"in_{k}", v.shape, mybir.dt.from_np(v.dtype), kind="ExternalInput").ap() for k, v in arrays.items()]
    out = nc.dram_tensor("out", (NN, D), FP, kind="ExternalOutput").ap()
    gnn_program(nc, *args, out)
    result = run(nc, [{f"in_{k}": v for k, v in arrays.items()}], core_ids=[0])
    return result.results[0]["out"][:N]
```

```python
import concourse.bass as bass
from concourse import mybir
from contextlib import ExitStack

P = 128
N, E, D = 6250, 200000, 16
U = 28
R = 14
A = U - R
G = 7
K = -(-E // (P * 2 * U)) * 2 * U
NB = -(-(N + 1) // P)
NN = P * NB
NG = K // U
AG = K // G
DD = D * D
TW = 3 * DD
BIG = 1e38
OOB = float(1 << 20)
POISON = 1e30
TINY = 1e-30
EPS = 1e-5
DC = 7
Q = 7
QW = Q * D
DW = DC * D
NCH = NB // DC
PB = 4
assert NB % DC == 0 and K % (2 * G) == 0 and NG >= NB and G * D == DW
CONT, BOTH, CONT_NEG, BOTH_NEG = range(4)

assert NB == Q * Q and PB * QW <= 512 and R <= 4 * PB and K % DW == 0

FP = mybir.dt.float32
BF = mybir.dt.bfloat16
HF = mybir.dt.float16
I32 = mybir.dt.int32
ALU = mybir.AluOpType
ACT = mybir.ActivationFunctionType
AX = mybir.AxisListType


def gnn_program(nc, x, src, dst, ew, ew1, ef, wpad, ident, dense_w, biases, eps, out):
    es = ExitStack()

    def sb(name, shape, dt=FP):
        return es.enter_context(nc.sbuf_tensor(name, shape, dt))

    def sem(name):
        return es.enter_context(nc.semaphore(name))

    def ring(name):
        return [sem(f"{name}_{i}") for i in range(2)]

    def dram(name, shape):
        return nc.dram_tensor(name, shape, FP).ap()

    with es:
        feat = [x] + [dram(f"feat{i}", (NN, D)) for i in range(1, 5)]
        run_tab = [dram(f"run_tab{i}", (P * K, D)) for i in range(4)]
        att_tab = dram("att_tab", (NN, TW))
        quot_tab = nc.dram_tensor("quot_tab", (K, P), HF).ap()

        idm = sb("idm", [P, P])
        ones = sb("ones", [P, P])
        edgei = sb("edgei", [P, 3], I32)
        edgef = sb("edgef", [P, 3])
        resets = sb("resets", [P, 2, K])
        neg, keep = resets[:, 0, :], resets[:, 1, :]
        scat = sb("scat", [P, K])
        nidi = sb("nidi", [P, NG + 1], I32)
        nid = sb("nid", [P, NG + 1])
        pidx = sb("pidx", [P, NG])
        cle = sb("cle", [P, NG])
        clt = sb("clt", [P, NG])
        full = sb("full", [P, NB])
        endf = sb("endf", [P, NB])
        endi = sb("endi", [P, NB], I32)
        counti = sb("counti", [P, 2, Q], I32)
        count = sb("count", [P, 2, Q])
        rem = sb("rem", [P, K], BF)
        fcol = sb("fcol", [P, 5])
        fidx = sb("fidx", [P, 3], I32)
        diag = sb("diag", [P, 3, P])
        frow = sb("frow", [P, P])
        rows = sb("rows", [P, 4, P])

        sidx = sb("sidx", [P, 2, U], I32)
        wts = sb("wts", [P, 2, U])
        msg = sb("msg", [P, 2, U, D])
        val = sb("val", [P, 2, U, D])
        run = sb("run", [P, 2, U, D])
        mring = sb("mring", [P, 2, U])
        pring = sb("pring", [P, 2], I32)
        parts = sb("parts", [P, NB, 3, D], BF)
        amask = sb("amask", [P, R, Q])
        tailT = sb("tailT", [D, P])
        carryT = sb("carryT", [D, P])
        lead = sb("lead", [P, D])
        lead2 = sb("lead2", [P, D])

        aidx = sb("aidx", [P, 2, G], I32)
        efs = sb("efs", [P, 2, G * D])
        efT = sb("efT", [P, 2, P])
        hsrc = sb("hsrc", [P, 2, G, D])
        wsb = sb("wsb", [P, G, 2 * DD])
        aring = sb("aring", [P, 2, 2, G])
        scidx = sb("scidx", [P, 2, G], I32)
        dbuf = sb("dbuf", [P, 2, G + 1, DD])
        bbuf = sb("bbuf", [P, 2, G + 1, 2, DD])
        amax = sb("amax", [P, 2, G, DD])
        smax = sb("smax", [P, G - 1, DD])
        st = sb("st", [P, 2, G, TW])
        stt = sb("stt", [P, 2, DD])
        ab = sb("ab", [P, 2, 2, P])
        slices = amax[:].rearrange("p a g c -> p (a g c)")[:, 0:2 * K].rearrange("p (a k) -> p a k", a=2).bitcast(I32)
        dsti = slices[:, 0, :]
        dstf = bbuf[:].rearrange("p a g t c -> p (a g t c)")[:, 0:K + 2]
        srci = slices[:, 1, :]
        raw = dbuf[:].rearrange("p a g c -> p (a g c)")
        quot = raw[:, 0:R * P].bitcast(HF)[:, 0:2 * R * P].rearrange("p (a e) -> p a e", a=2)
        picked = raw[:, R * P:R * P + R * QW].rearrange("p (r q c) -> p r q c", q=Q, c=D)
        quotT = raw[:, 0:(K // DW) * P // 2].bitcast(HF).rearrange("p (c q) -> p c q", q=P)
        flat = st[:].rearrange("p a g c -> p (a g c)")
        hot = [t[:, 0:Q * R * P // 2].bitcast(BF).rearrange("p (m e) -> p m e", m=Q)
               for t in (bbuf[:].rearrange("p a g t c -> p (a g t c)"), flat)]
        junk = flat[:, Q * R * P // 2:Q * R * P // 2 + K]
        quotf = flat[:, 0:K]
        compared = flat[:, 0:NG * P].rearrange("p (b q) -> p b q", b=NG)

        x0 = sb("x0", [P, NB, D])
        xa = sb("xa", [P, NB, D])
        xb = sb("xb", [P, NB, D])
        got = sb("got", [P, NB, D])
        nt = sb("nt", [P, NB, D])
        nu = sb("nu", [P, NB, D])
        zt = got[:].rearrange("p b c -> p (b c)")[:, 0:TW]
        tT = nt[:].rearrange("p b c -> p (b c)")[:, 0:6 * P].rearrange("p (t q) -> p t q", q=P)
        cT = nu[:].rearrange("p b c -> p (b c)")[:, 0:6 * P].rearrange("p (t q) -> p t q", q=P)
        vT = sb("vT", [P, NCH, P])
        bd = sb("bd", [P, 5, DW])
        bias = sb("bias", [P, 5, D])
        epsb = sb("epsb", [P, 2])
        st1 = sb("st1", [P, NB])
        st2 = sb("st2", [P, NB])
        st3 = sb("st3", [P, NB])
        bad = sb("bad", [P, NB])

        ps = es.enter_context(nc.psum_tensor("ps", [P, 8, 512], FP))

        s_const = sem("s_const")
        s_zero = sem("s_zero")
        s_quot = sem("s_quot")
        s_quots = sem("s_quots")
        s_parts = sem("s_parts")
        s_w = sem("s_w")
        s_tab = sem("s_tab")
        s_iota = sem("s_iota")
        s_chain = sem("s_chain")
        s_loop = sem("s_loop")
        s_diag = sem("s_diag")
        s_rows = sem("s_rows")
        s_pidx = ring("s_pidx")
        s_slice = ring("s_slice")
        s_count = ring("s_count")
        s_pool = sem("s_pool")
        s_sp = sem("s_sp")
        s_idxr = sem("s_idxr")
        s_fixed = sem("s_fixed")
        s_node = [sem(f"s_node{i}") for i in range(4)]
        s_tail = sem("s_tail")
        s_turn = sem("s_turn")
        s_car = sem("s_car")
        s_back = sem("s_back")
        s_lead = sem("s_lead")
        s_att = ring("s_att")
        s_attu = sem("s_attu")
        s_feat = sem("s_feat")
        s_feats = sem("s_feats")
        s_din = sem("s_din")
        s_dtr = sem("s_dtr")
        s_dcp = sem("s_dcp")
        s_dmm = sem("s_dmm")
        s_asked = sem("s_asked")
        s_acted = sem("s_acted")
        s_out = sem("s_out")
        NARROW = ("idx", "w", "quot", "hot", "pick", "read", "got", "mul", "act", "run", "put")
        narrow = [{k: ring(f"n{n}_{k}") for k in NARROW} for n in range(4)]
        a_idx = ring("a_idx")
        a_ef = ring("a_ef")
        a_got = ring("a_got")
        a_tr = ring("a_tr")
        a_trs = ring("a_trs")
        a_mm = ring("a_mm")
        a_read = ring("a_read")
        a_d = ring("a_d")
        a_exp = ring("a_exp")
        a_max = ring("a_max")
        a_st = ring("a_st")
        a_sc = ring("a_sc")

        HALF = NG // 2
        AHALF = AG // 2
        block = es.enter_context(nc.Block())

        @block.sync
        def _(sp):
            def narrow_pass(n):
                q = narrow[n]
                table = run_tab[n].rearrange("(p k) c -> p (k c)", p=P)

                def load(g, s):
                    sp.dma_start(sidx[:, s, :], src[:, bass.ds(g * U, U)]).then_inc(q["idx"][s], 16)
                    if n < 2:
                        sp.dma_start(wts[:, s, :], (ew, ew1)[n][:, bass.ds(g * U, U)]).then_inc(q["w"][s], 16)

                def load_quot(g, s):
                    sp.dma_start(quot[:, s, :], quot_tab.rearrange("k q -> (k q)")[bass.ds((g * U + A) * P, R * P)]
                                 .partition_broadcast(P)).then_inc(q["quot"][s], 16)

                def round_(j, more, more_quot):
                    for s in range(2):
                        sp.wait_ge(q["run"][s], j + 1)
                        sp.sem_inc(s_sp, 1)
                        sp.dma_start(table[:, bass.ds((2 * j + s) * (U * D), U * D)],
                                     run[:, s].rearrange("p u c -> p (u c)")).then_inc(q["put"][s], 16)
                        if more:
                            load(2 * j + 2 + s, s)
                        if more_quot or (more and s == 0):
                            sp.wait_ge(q["hot"][1 - s], j + 1 + s)
                            sp.sem_inc(s_sp, 1)
                            load_quot(2 * j + 3 + s, 1 - s)

                for s in range(2):
                    load(s, s)
                if n == 0:
                    sp.wait_ge(s_quots, 16)
                for s in range(2):
                    load_quot(s, s)
                sp.wait_ge(q["hot"][0], 1)
                load_quot(2, 0)
                with sp.Fori(0, HALF - 2) as j:
                    round_(j, True, True)
                round_(HALF - 2, True, False)
                round_(HALF - 1, False, False)

            def put_feat(i, tile):
                sp.wait_ge(s_feat, i)
                sp.dma_start(feat[i].rearrange("(p b) c -> p (b c)", p=P),
                             tile[:].rearrange("p b c -> p (b c)")).then_inc(s_feats, 16)

            def attention():
                def load(g, s):
                    sp.dma_start(aidx[:, s, :], src[:, bass.ds(g * G, G)]).then_inc(a_idx[s], 16)
                    sp.dma_start(efs[:, s, :], ef[:, bass.ds(g * (G * D), G * D)]).then_inc(a_ef[s], 16)

                for s in range(2):
                    load(s, s)
                with sp.Fori(0, AHALF - 1) as j:
                    for s in range(2):
                        sp.wait_ge(a_tr[s], j + 1)
                        sp.sem_inc(s_sp, 1)
                        sp.wait_ge(a_got[s], (j + 1) * (16 * G))
                        sp.sem_inc(s_sp, 1)
                        load(2 * j + 2 + s, s)
                states = att_tab.rearrange("(p b) c -> p b c", p=P)
                sp.wait_ge(s_fixed, 16 * 4)
                for c in range(NCH):
                    if c >= 2:
                        sp.wait_ge(s_attu, c - 1)
                    sp.dma_start(bbuf[:, c % 2, 0:DC].rearrange("p b t c -> p b (t c)"),
                                 states[:, c * DC:(c + 1) * DC, 0:2 * DD]).then_inc(s_att[c % 2], 16)

            narrow_pass(0)
            put_feat(1, xa)
            attention()
            put_feat(2, xb)
            narrow_pass(1)
            put_feat(3, xa)
            narrow_pass(2)
            put_feat(4, xb)
            narrow_pass(3)
            sp.wait_ge(s_feat, 5)
            sp.dma_start(out.rearrange("(p b) c -> p (b c)", p=P),
                         nt[:].rearrange("p b c -> p (b c)")).then_inc(s_out, 16)
            sp.wait_ge(s_out, 16)

        @block.gpsimd
        def _(pool):
            def rows_at(ap):
                return bass.IndirectOffsetOnAxis(ap=ap, axis=0)

            def gather(dest, table, idx):
                return pool.indirect_dma_start(dest, None, table, rows_at(idx))

            def scatter(table, idx, source, **kw):
                return pool.indirect_dma_start(table, rows_at(idx), source, None, **kw)

            def narrow_pass(n, table):
                q = narrow[n]
                used = q["mul"] if n < 2 else q["run"]
                with pool.Fori(0, HALF) as j:
                    for s in range(2):
                        pool.wait_ge(q["idx"][s], 16 * (j + 1))
                        pool.wait_ge(used[s], j)
                        pool.sem_inc(s_pool, 1)
                        for u in range(A):
                            gather(msg[:, s, u, :], table, sidx[:, s, u:u + 1]).then_inc(q["got"][s], 16)
                        if n == 0:
                            pool.wait_ge(s_pidx[s], j + 1)
                            pool.sem_inc(s_pool, 1)
                            gather(slices[:, s, :], dst, pring[:, s:s + 1]).then_inc(s_slice[s], 16)
                if n == 0:
                    pool.wait_ge(s_idxr, 1)
                for s in range(2):
                    pool.wait_ge(q["put"][s], 16 * HALF)
                fixes = 2 * n if n == 0 else 2 * n + 2
                gather(lead[:], run_tab[n], fidx[:, 0:1]).then_inc(s_fixed, 16)
                pool.wait_ge(s_lead, fixes // 2 + 1)
                scatter(run_tab[n], fidx[:, 0:1], lead2[:]).then_inc(s_fixed, 16)
                pool.wait_ge(s_fixed, 16 * (fixes + 2))
                if n == 0:
                    pool.wait_ge(s_tab, 16)
                for b in range(NB):
                    gather(got[:, b, :], run_tab[n], endi[:, b:b + 1]).then_inc(s_node[n], 16)

            def attention():
                def group(j, s, store):
                    pool.wait_ge(a_idx[s], 16 * (j + 1))
                    pool.wait_ge(a_read[s], j)
                    pool.sem_inc(s_pool, 1)
                    for k in range(G):
                        gather(hsrc[:, s, k, :], feat[1], aidx[:, s, k:k + 1]).then_inc(a_got[s], 16)
                    if store:
                        put(j, s)

                def put(j, s):
                    pool.wait_ge(a_st[s], j)
                    pool.sem_inc(s_pool, 1)
                    for k in range(G):
                        scatter(att_tab, scidx[:, s, k:k + 1], st[:, s, k, :],
                                bounds_check=NN - 1, oob_is_err=False).then_inc(a_sc[s], 16)

                pool.wait_ge(s_tab, 16)
                for s in range(2):
                    group(0, s, False)
                with pool.Fori(1, AHALF) as j:
                    for s in range(2):
                        group(j, s, True)
                for s in range(2):
                    put(AHALF, s)
                for s in range(2):
                    pool.wait_ge(a_sc[s], 16 * G * AHALF)
                pool.wait_ge(s_tail, 2)
                gather(st[:, 0, 0, :], att_tab, fidx[:, 1:2]).then_inc(s_fixed, 16)
                pool.wait_ge(s_lead, 2)
                scatter(att_tab, fidx[:, 2:3], st[:, 0, 1, :],
                        bounds_check=NN - 1, oob_is_err=False).then_inc(s_fixed, 16)

            pool.memset(bd[:], 0.0).then_inc(s_zero, 1)
            pool.memset(wsb[:], 0.0).then_inc(s_zero, 1)
            pool.memset(zt, 0.0).then_inc(s_zero, 1)
            pool.memset(efT[:], 1.0).then_inc(s_zero, 1)
            pool.memset(ones[:], 1.0).then_inc(s_zero, 1)
            pool.iota(nidi[:, 0:NG], [[1, NG]], base=0, channel_multiplier=NB).then_inc(s_iota, 1)
            pool.iota(nidi[:, NG:NG + 1], [[0, 1]], base=-1, channel_multiplier=K).then_inc(s_iota, 1)
            pool.iota(counti[:, 0, :], [[1, Q]], base=0, channel_multiplier=Q).then_inc(s_iota, 1)
            pool.iota(counti[:, 1, :], [[1, Q]], base=0, channel_multiplier=0).then_inc(s_iota, 1)
            narrow_pass(0, feat[0])
            pool.wait_ge(s_feats, 16)
            attention()
            for n in range(1, 4):
                pool.wait_ge(s_feats, 16 * (n + 1))
                narrow_pass(n, feat[n + 1])

        @block.scalar
        def _(act):
            acted = [0]

            def asked(dest, source, func):
                acted[0] += 1
                act.wait_ge(s_asked, acted[0])
                nc.scalar.activation(dest, source, func).then_inc(s_acted, 1)

            def dense(i):
                act.wait_ge(s_dtr, i + 1)
                nc.scalar.activation(vT[0:DW, 0:PB, :], ps[0:DW, 0, 0:PB * P].rearrange("p (c q) -> p c q", q=P), ACT.Copy)
                nc.scalar.activation(vT[0:DW, PB:NCH, :], ps[0:DW, 1, 0:(NCH - PB) * P].rearrange("p (c q) -> p c q", q=P),
                                     ACT.Copy).then_inc(s_dcp, 1)

            act.dma_start(srci, src).then_inc(s_const, 16)
            act.dma_start(idm[:], ident).then_inc(s_const, 16)
            act.dma_start(dsti, dst[1:P + 1, :]).then_inc(s_const, 16)
            for c, (r, k) in enumerate(((0, K - 1), (0, 0), (2, 0))):
                act.dma_start(edgei[:, c:c + 1], dst[r:r + P, k:k + 1], allow_slow_non_contiguous=True).then_inc(s_const, 16)
            act.dma_start(x0[:].rearrange("p b c -> p (b c)"), x.rearrange("(p b) c -> p (b c)", p=P)).then_inc(s_const, 16)
            for i in range(2):
                act.dma_start(epsb[:, i:i + 1], eps[i:i + 1].partition_broadcast(P)).then_inc(s_const, 16)
            for i in range(5):
                act.dma_start(bias[:, i, :], biases[i].partition_broadcast(P)).then_inc(s_const, 16)
            act.wait_ge(s_quot, 3)
            act.dma_start(quot_tab.rearrange("(c r) q -> r c q", r=DW), quotT[0:DW]).then_inc(s_quots, 16)
            act.wait_ge(s_zero, 3)
            for i in range(5):
                for c in range(DC):
                    act.dma_start(bd[c * D:(c + 1) * D, i, c * D:(c + 1) * D], dense_w[i]).then_inc(s_w, 16)
            for c in range(G):
                act.dma_start(wsb[c * D:(c + 1) * D, c, :], wpad[0:D, :]).then_inc(s_w, 16)
                act.dma_start(wsb[DW:DW + 1, c, :], wpad[D:D + 1, :]).then_inc(s_w, 16)
            act.dma_start(att_tab.rearrange("(p b) c -> p b c", p=P),
                          zt.unsqueeze(1).to_broadcast([P, NB, TW])).then_inc(s_tab, 16)
            q = narrow[0]
            with act.Fori(0, HALF) as j:
                for s in range(2):
                    act.wait_ge(q["mul"][s], j + 1)
                    nc.scalar.activation(val[:, s], val[:, s], ACT.Tanh).then_inc(q["act"][s], 1)
            asked(st3[:], st2[:], ACT.Sqrt)

            act.wait_ge(s_zero, 4)

            def turn_copy(j, s):
                act.wait_ge(a_tr[s], j + 1)
                nc.scalar.activation(efT[0:DW, s, :], ps[0:DW, G, 0:P], ACT.Copy).then_inc(a_trs[s], 1)

            def group(j, s, more, old):
                if more:
                    turn_copy(j + s, 1 - s)
                act.wait_ge(a_d[s], j + 1)
                nc.scalar.activation(bbuf[:, s, :, 0, :], dbuf[:, s], ACT.Exp).then_inc(a_exp[s], 1)
                if old:
                    act.wait_ge(a_sc[s], j * (16 * G))
                nc.scalar.activation(st[:, s, :, 2 * DD:TW], amax[:, s], ACT.Copy).then_inc(a_max[s], 1)

            turn_copy(0, 0)
            for s in range(2):
                group(0, s, True, False)
            with act.Fori(1, AHALF - 1) as j:
                for s in range(2):
                    group(j, s, True, True)
            group(AHALF - 1, 0, True, True)
            group(AHALF - 1, 1, False, True)
            asked(ab[:], ab[:], ACT.Exp)
            asked(bbuf[:, 0, 0], bbuf[:, 0, 0], ACT.Exp)
            asked(st3[:], st2[:], ACT.Sqrt)
            dense(0)
            asked(st3[:], st2[:], ACT.Sqrt)
            for i in range(1, 5):
                dense(i)
            asked(nu[:], nt[:], ACT.Exp)
            asked(st2[:], st1[:], ACT.Ln)
            asked(st3[:], st2[:], ACT.Sqrt)

        @block.tensor
        def _(pe):
            def carry(i, tail):
                pe.wait_ge(s_tail, 1 + i)
                m = tail.shape[1]
                for c in range(-(-m // P)):
                    w = min(P, m - c * P)
                    last = nc.tensor.transpose(ps[0:w, c // PB, (c % PB) * P:(c % PB + 1) * P], tail[:, c * P:c * P + w], idm[:])
                last.then_inc(s_turn, 1)
                pe.wait_ge(s_car, 1 + i)
                for c in range(-(-m // P)):
                    w = min(P, m - c * P)
                    source = cT[:, c, :] if m > P else carryT[:]
                    last = nc.tensor.transpose(ps[:, 2 + c // PB, (c % PB) * P:(c % PB) * P + w], source, idm[0:w, 0:w])
                last.then_inc(s_back, 1)

            def dense(i, w, v):
                pe.wait_ge(s_din, i + 1)
                for c in range(NCH):
                    last = nc.tensor.transpose(ps[0:DW, c // PB, (c % PB) * P:(c % PB + 1) * P],
                                               v[:, c * DC:(c + 1) * DC, :].rearrange("p b c -> p (b c)"), idm[:])
                last.then_inc(s_dtr, 1)
                pe.wait_ge(s_dcp, i + 1)
                for c in range(NCH):
                    last = nc.tensor.matmul(ps[:, 2 + c // PB, (c % PB) * DW:(c % PB + 1) * DW], vT[0:DW, c, :], bd[0:DW, w, :],
                                            start=True, stop=True)
                last.then_inc(s_dmm, 1)

            def narrow_pass(n):
                q = narrow[n]
                pe.wait_ge(s_parts, n + 1)

                def fetch(j, s):
                    pe.wait_ge(q["hot"][s], j + 1)
                    pe.wait_ge(q["read"][s], j)
                    for t in range(R):
                        for m in range(Q):
                            for part in range(3):
                                last = nc.tensor.matmul(
                                    ps[:, 4 * s + t // PB, (t % PB) * QW:(t % PB + 1) * QW].rearrange("p (q c) -> p q c", c=D),
                                    hot[s][:, m, t * P:(t + 1) * P], parts[:, m * Q:(m + 1) * Q, part, :],
                                    start=m == 0 and part == 0, stop=m == Q - 1 and part == 2)
                    last.then_inc(q["pick"][s], 1)

                with pe.Fori(0, HALF) as j:
                    for s in range(2):
                        fetch(j, s)

            pe.wait_ge(s_const, 16 * 2)
            pe.wait_ge(s_quot, 1)
            for c in range(K // DW):
                last = nc.tensor.transpose(ps[0:DW, c // PB, (c % PB) * P:(c % PB + 1) * P], quotf[:, c * DW:(c + 1) * DW], idm[:])
            last.then_inc(s_quot, 1)
            pe.wait_ge(s_zero, 5)
            pe.wait_ge(s_diag, 1)
            nc.tensor.matmul(ps[:, 4, 0:3 * P], ones[:], diag[:].rearrange("p a q -> p (a q)"), start=True, stop=True).then_inc(s_rows, 1)
            tail = run[:, 1, U - 1, :]
            narrow_pass(0)
            carry(0, tail)

            pe.wait_ge(s_w, 16 * (5 * DC + 2 * G))

            def turn(j, s):
                pe.wait_ge(a_ef[s], 16 * (j + 1))
                nc.tensor.transpose(ps[0:DW, G, 0:P], efs[:, s, :], idm[:]).then_inc(a_tr[s], 1)

            def group(j, s, more, old):
                pe.wait_ge(a_trs[s], j + 1)
                if more:
                    turn(j + s, 1 - s)
                if old:
                    pe.wait_ge(a_read[1 - s], j + s)
                for k in range(G):
                    last = nc.tensor.matmul(ps[:, k, :], efT[0:DW + 1, s, :], wsb[0:DW + 1, k, :], start=True, stop=True)
                last.then_inc(a_mm[s], 1)

            pe.wait_ge(s_feat, 1)
            turn(0, 0)
            group(0, 0, True, False)
            group(0, 1, True, True)
            with pe.Fori(1, AHALF - 1) as j:
                for s in range(2):
                    group(j, s, True, True)
            group(AHALF - 1, 0, True, True)
            group(AHALF - 1, 1, False, True)
            carry(1, st[:, 1, G - 1, :])
            narrow_pass(1)
            carry(2, tail)
            dense(0, 0, nt)
            narrow_pass(2)
            carry(3, tail)
            dense(1, 1, nt)
            dense(2, 2, nt)
            narrow_pass(3)
            carry(4, tail)
            dense(3, 3, nt)
            dense(4, 4, nt)

        @block.vector
        def _(dve):
            v = nc.vector
            chained = [0]
            looped = [0]

            def link(ins):
                chained[0] += 1
                ins.then_inc(s_chain, 1)
                dve.wait_ge(s_chain, chained[0])

            def loop_start():
                looped[0] = 0
                dve.sem_clear(s_loop)

            def hold(ins):
                looped[0] += 1
                ins.then_inc(s_loop, 1)
                dve.wait_ge(s_loop, looped[0])

            def wide(ap):
                return ap.unsqueeze(2).to_broadcast([P, ap.shape[1], D])

            def everywhere(row):
                return row.unsqueeze(1).to_broadcast([P, NB, D])

            def tt(dest, a, b, op):
                return v.tensor_tensor(dest, a, b, op)

            asks = [0]

            def ask(ins):
                asks[0] += 1
                ins.then_inc(s_asked, 1)
                dve.wait_ge(s_acted, asks[0])

            def split(features):
                link(v.tensor_copy(parts[:, :, 0, :], features[:]))
                link(tt(nt[:], features[:], parts[:, :, 0, :], ALU.subtract))
                link(v.tensor_copy(parts[:, :, 1, :], nt[:]))
                link(tt(nt[:], nt[:], parts[:, :, 1, :], ALU.subtract))
                v.tensor_copy(parts[:, :, 2, :], nt[:]).then_inc(s_parts, 1)

            dve.wait_ge(s_const, 16 * 14)
            dve.wait_ge(s_iota, 4)
            link(v.tensor_copy(count[:], counti[:]))
            srcf, trial = dstf[:, 0:K], junk
            link(v.tensor_copy(srcf, srci))
            link(v.tensor_scalar(srci, srcf, 1.0 / Q, None, ALU.mult))
            link(v.tensor_copy(quotf, srci))
            link(v.scalar_tensor_tensor(trial, quotf, -float(Q), srcf, ALU.mult, ALU.add))
            over = scat[:]
            link(v.tensor_scalar(over, trial, Q - 0.5, None, ALU.is_gt))
            link(tt(quotf, quotf, over, ALU.add))
            link(v.tensor_scalar(over, trial, 0.0, None, ALU.is_lt))
            link(tt(quotf, quotf, over, ALU.subtract))
            v.scalar_tensor_tensor(rem[:], quotf, -float(Q), srcf, ALU.mult, ALU.add).then_inc(s_quot, 1)
            dve.wait_ge(s_quot, 2)
            for b in range(4):
                chunks = min(PB, K // DW - b * PB)
                last = v.tensor_copy(quotT[0:DW, b * PB:b * PB + chunks, :],
                                     ps[0:DW, b, 0:chunks * P].rearrange("p (c q) -> p c q", q=P))
            last.then_inc(s_quot, 1)
            dve.wait_ge(s_quots, 16)
            link(v.tensor_copy(dstf[:, 1:K + 1], dsti))
            link(v.tensor_copy(edgef[:], edgei[:]))
            link(v.tensor_copy(dstf[:, 0:1], edgef[:, 0:1]))
            link(v.tensor_copy(dstf[:, K + 1:K + 2], edgef[:, 2:3]))
            link(v.tensor_copy(nid[:], nidi[:]))
            first = dstf[:, 1:2]
            link(tt(fcol[:, 0:1], first, dstf[:, 0:1], ALU.is_equal))
            link(tt(fcol[:, 1:2], edgef[:, 0:1], edgef[:, 1:2], ALU.is_equal))
            link(tt(fcol[:, 1:2], fcol[:, 0:1], fcol[:, 1:2], ALU.mult))
            link(v.tensor_scalar(diag[:, 0, :], idm[:], first, None, ALU.mult))
            link(v.tensor_scalar(diag[:, 1, :], idm[:], fcol[:, 0:1], None, ALU.mult))
            v.tensor_scalar(diag[:, 2, :], idm[:], fcol[:, 1:2], None, ALU.mult).then_inc(s_diag, 1)
            split(x0)
            link(tt(keep, dstf[:, 1:K + 1], dstf[:, 0:K], ALU.is_equal))
            link(v.memset(keep[:, 0:1], 0.0))
            link(v.tensor_scalar(neg, keep, 1.0, BIG, ALU.subtract, ALU.mult))
            link(tt(scat[:], dstf[:, 1:K + 1], dstf[:, 2:K + 2], ALU.is_equal))
            link(v.scalar_tensor_tensor(scat[:], scat[:], OOB, dstf[:, 1:K + 1], ALU.mult, ALU.add))
            link(v.tensor_scalar(junk, dstf[:, 1:K + 1], first, 0.0, ALU.is_equal, ALU.add, accum_out=fcol[:, 2:3]))
            link(tt(fidx[:, 0:1], fcol[:, 2:3], nid[:, NG:NG + 1], ALU.add))
            link(v.tensor_copy(fidx[:, 1:2], first))
            link(tt(fcol[:, 3:4], first, dstf[:, K + 1:K + 2], ALU.is_equal))
            link(v.tensor_scalar(fcol[:, 3:4], fcol[:, 3:4], -1.0, 1.0, ALU.mult, ALU.add))
            link(tt(fcol[:, 3:4], fcol[:, 3:4], fcol[:, 0:1], ALU.mult))
            link(v.tensor_scalar(fcol[:, 3:4], fcol[:, 3:4], -OOB, OOB, ALU.mult, ALU.add))
            link(tt(fidx[:, 2:3], fcol[:, 3:4], first, ALU.add))
            dve.wait_ge(s_rows, 1)
            link(v.tensor_copy(frow[:], ps[:, 4, 0:P]))
            link(v.tensor_copy(rows[:, 0:2, :], ps[:, 4, P:3 * P].rearrange("p (a q) -> p a q", q=P)))
            link(v.tensor_scalar(rows[:, 2:4, :], rows[:, 0:2, :], 1.0, BIG, ALU.subtract, ALU.mult))
            link(tt(compared, frow[:].unsqueeze(1).to_broadcast([P, NG, P]),
                    nid[:, 0:NG].unsqueeze(2).to_broadcast([P, NG, P]), ALU.is_le))
            link(v.tensor_reduce(pidx[:], compared, AX.X, ALU.add))
            link(v.tensor_scalar(pidx[:], pidx[:], 1.0, None, ALU.max))

            def narrow_pass(n):
                q = narrow[n]
                most = n == 1
                mask = neg if most else keep

                def next_slice(g, s):
                    v.tensor_copy(pring[:, s:s + 1], pidx[:, bass.ds(g, 1)]).then_inc(s_pidx[s], 1)

                def one_hots(j, s):
                    dve.wait_ge(q["quot"][s], 16 * (j + 1))
                    dve.wait_ge(q["pick"][s], j)
                    for m in range(Q):
                        last = v.tensor_scalar(hot[s][:, m, :], quot[:, s, :], count[:, 0, m:m + 1], None, ALU.is_equal)
                    last.then_inc(q["hot"][s], 1)

                def pick(j, s):
                    hold(tt(amask[:], rem[:, bass.ds((2 * j + s) * U + A, R)].unsqueeze(2).to_broadcast([P, R, Q]),
                            count[:, 1, :].unsqueeze(1).to_broadcast([P, R, Q]), ALU.is_equal))
                    dve.wait_ge(q["pick"][s], j + 1)
                    for b in range(-(-R // PB)):
                        steps = min(PB, R - b * PB)
                        last = tt(picked[:, b * PB:b * PB + steps],
                                  ps[:, 4 * s + b, 0:steps * QW].rearrange("p (r q c) -> p r q c", q=Q, c=D),
                                  amask[:, b * PB:b * PB + steps].unsqueeze(3).to_broadcast([P, steps, Q, D]), ALU.mult)
                    last.then_inc(q["read"][s], 1)
                    dve.wait_ge(q["read"][s], j + 1)
                    hold(v.tensor_reduce(msg[:, s, A:U, :], picked.rearrange("p r q c -> p r c q"), AX.X, ALU.add))

                def round_(j, more):
                    loop_start()
                    for s in range(2):
                        g = 2 * j + s
                        if more or s == 0:
                            one_hots(j + s, 1 - s)
                        pick(j, s)
                        hold(v.tensor_copy(mring[:, s, :], mask[:, bass.ds(g * U, U)]))
                        dve.wait_ge(q["got"][s], (j + 1) * (16 * A))
                        values = msg
                        if n < 2:
                            dve.wait_ge(q["w"][s], 16 * (j + 1))
                            tt(val[:, s], msg[:, s], wts[:, s, :].unsqueeze(2).to_broadcast([P, U, D]),
                               ALU.mult).then_inc(q["mul"][s], 1)
                            values = val
                            dve.wait_ge(q["act"][s] if n == 0 else q["mul"][s], j + 1)
                        dve.wait_ge(q["put"][s], 16 * j)
                        for c in range(D):
                            last = v.tensor_tensor_scan(run[:, s, :, c], mring[:, s, :], values[:, s, :, c], run[:, 1 - s, U - 1, c:c + 1],
                                                        ALU.add if most else ALU.mult, ALU.max if most else ALU.add)
                        last.then_inc(q["run"][s], 1)
                        dve.wait_ge(q["run"][s], j + 1)
                        if n == 0:
                            dve.wait_ge(s_slice[s], 16 * (j + 1))
                            node = nid[:, bass.ds(g, 1)]
                            hold(v.tensor_scalar(junk, slices[:, s, :], node, 0.0, ALU.is_le, ALU.add,
                                                 accum_out=cle[:, bass.ds(g, 1)]))
                            hold(v.tensor_scalar(junk, slices[:, s, :], node, 0.0, ALU.is_lt, ALU.add,
                                                 accum_out=clt[:, bass.ds(g, 1)]))
                            if more:
                                next_slice(g + 2, s)

                link(v.memset(run[:, 1, U - 1, :], 0.0))
                if n == 0:
                    for s in range(2):
                        next_slice(s, s)
                one_hots(0, 0)
                with dve.Fori(0, HALF - 1) as j:
                    round_(j, True)
                round_(HALF - 1, False)
                if n == 0:
                    link(v.tensor_scalar(endf[:], pidx[:, 0:NB], -1.0, float(K), ALU.add, ALU.mult))
                    link(tt(endf[:], endf[:], cle[:, 0:NB], ALU.add))
                    link(v.tensor_scalar(endf[:], endf[:], -1.0, 0.0, ALU.add, ALU.max))
                    link(tt(full[:], clt[:, 0:NB], cle[:, 0:NB], ALU.is_lt))
                    link(v.tensor_scalar(st1[:], nid[:, 0:NB], float(N), None, ALU.is_ge))
                    link(tt(full[:], full[:], st1[:], ALU.max))
                    v.tensor_copy(endi[:], endf[:]).then_inc(s_idxr, 1)
                i = 0 if n == 0 else n + 1
                v.memset(tailT[:, 0:1], -BIG if most else 0.0).then_inc(s_tail, 1)
                dve.wait_ge(s_turn, i + 1)
                link(tt(tailT[:, 1:P], ps[0:D, 0, 0:P - 1], rows[0:D, CONT_NEG if most else CONT, 1:P], ALU.add if most else ALU.mult))
                v.tensor_tensor_scan(carryT[:], rows[0:D, BOTH_NEG if most else BOTH, :], tailT[:], 0.0,
                                     ALU.add if most else ALU.mult, ALU.max if most else ALU.add).then_inc(s_car, 1)
                dve.wait_ge(s_back, i + 1)
                dve.wait_ge(s_fixed, 16 * (2 * i + 1))
                tt(lead2[:], lead[:], ps[:, 2, 0:D], ALU.max if most else ALU.add).then_inc(s_lead, 1)
                dve.wait_ge(s_node[n], 16 * NB)

            def layer_norm(dest, source):
                link(v.tensor_reduce(st1[:], source[:], AX.X, ALU.add))
                link(v.tensor_scalar(st1[:], st1[:], 1.0 / D, None, ALU.mult))
                link(tt(nt[:], source[:], wide(st1[:]), ALU.subtract))
                link(tt(nu[:], nt[:], nt[:], ALU.mult))
                link(v.tensor_reduce(st2[:], nu[:], AX.X, ALU.add))
                ask(v.tensor_scalar(st2[:], st2[:], 1.0 / D, EPS, ALU.mult, ALU.add))
                link(v.reciprocal(st3[:], st3[:]))
                return tt(dest[:], nt[:], wide(st3[:]), ALU.mult)

            def attention():
                link(v.memset(amax[:, 1, G - 1, :], 0.0))
                link(v.memset(st[:, 1, G - 1, 0:2 * DD], 0.0))

                def mark(ins):
                    looped[0] += 1
                    ins.then_inc(s_loop, 1)
                    return looped[0]

                def need(count):
                    dve.wait_ge(s_loop, count)

                def logits(j, s):
                    dve.wait_ge(a_got[s], (j + 1) * (16 * G))
                    dve.wait_ge(a_mm[s], j + 1)
                    return mark(times_source(s, 0, dbuf[:, s, 0:G, :]))

                def times_source(s, which, dest):
                    return tt(dest.rearrange("p g (i o) -> p g i o", o=D),
                              ps[:, 0:G, which * DD:(which + 1) * DD].rearrange("p g (i o) -> p g i o", o=D),
                              hsrc[:, s].unsqueeze(3).to_broadcast([P, G, D, D]), ALU.mult)

                def messages(s):
                    times_source(s, 1, bbuf[:, s, 0:G, 1, :]).then_inc(a_read[s], 1)

                def ring_copy(j, s):
                    return mark(v.tensor_copy(aring[:, s], resets[:, :, bass.ds((2 * j + s) * G, G)]))

                def running_max(s, k):
                    return mark(v.scalar_tensor_tensor(amax[:, s, k, :], amax[:, 1 - s, G - 1, :] if k == 0 else amax[:, s, k - 1, :],
                                                       aring[:, s, 0, k:k + 1], dbuf[:, s, k, :], ALU.add, ALU.max))

                def segment_max(s, k):
                    return mark(v.scalar_tensor_tensor(smax[:, k, :], amax[:, s, G - 1, :] if k == G - 2 else smax[:, k + 1, :],
                                                       aring[:, s, 0, k + 1:k + 2], amax[:, s, k, :], ALU.add, ALU.max))

                def differences(s, last):
                    tt(dbuf[:, s, G - 1, :], dbuf[:, s, G - 1, :], amax[:, s, G - 1, :], ALU.subtract)
                    need(last)
                    tt(dbuf[:, s, 0:G - 1, :], dbuf[:, s, 0:G - 1, :], smax[:], ALU.subtract)
                    v.scalar_tensor_tensor(dbuf[:, s, G, :], amax[:, 1 - s, G - 1, :], aring[:, s, 0, 0:1], smax[:, 0, :],
                                           ALU.add, ALU.subtract).then_inc(a_d[s], 1)

                def weighted(j, s):
                    dve.wait_ge(a_exp[s], j + 1)
                    return mark(tt(bbuf[:, s, 0:G, 1, :], bbuf[:, s, 0:G, 1, :], bbuf[:, s, 0:G, 0, :], ALU.mult))

                def rescaled(s):
                    return mark(tt(stt[:], st[:, 1 - s, G - 1, 0:2 * DD].rearrange("p (t c) -> p t c", t=2),
                                   bbuf[:, s, G, 0, :].unsqueeze(1).to_broadcast([P, 2, DD]), ALU.mult))

                def store_index(j, s):
                    v.tensor_copy(scidx[:, s, :], scat[:, bass.ds((2 * j + s) * G, G)])

                def running_sum(s, k):
                    if k == 0:
                        return mark(tt(st[:, s, 0, 0:2 * DD].rearrange("p (t c) -> p t c", t=2), stt[:], bbuf[:, s, 0, :, :], ALU.add))
                    return v.scalar_tensor_tensor(st[:, s, k, 0:2 * DD], st[:, s, k - 1, 0:2 * DD], aring[:, s, 1, k:k + 1],
                                                  bbuf[:, s, k, :, :].rearrange("p t c -> p (t c)"), ALU.mult, ALU.add)

                def slot_free(j, s, old):
                    if old:
                        dve.wait_ge(a_sc[s], j * (16 * G))
                    dve.wait_ge(a_max[s], j + 1)

                def step(j, s, old, jb, old_b):
                    b = 1 - s
                    if old:
                        dve.wait_ge(a_exp[s], j)
                    logits(j, s)
                    r = ring_copy(j, s)
                    if old:
                        dve.wait_ge(a_max[s], j)
                    need(r)
                    m = running_max(s, 0)
                    messages(s)
                    need(m)
                    m = running_max(s, 1)
                    w = weighted(jb, b)
                    need(m)
                    m = running_max(s, 2)
                    rescale = rescaled(b)
                    need(m)
                    m = running_max(s, 3)
                    slot_free(jb, b, old_b)
                    store_index(jb, b)
                    need(rescale)
                    t = running_sum(b, 0)
                    for k in range(4, G):
                        need(m)
                        m = running_max(s, k)
                        need(t)
                        t = mark(running_sum(b, k - 3))
                    for k in range(G - 2, G - 4, -1):
                        need(m)
                        m = segment_max(s, k)
                        need(t)
                        t = mark(running_sum(b, G + 2 - k))
                    need(m)
                    m = segment_max(s, G - 4)
                    need(t)
                    running_sum(b, G - 1).then_inc(a_st[b], 1)
                    for k in range(G - 5, -1, -1):
                        need(m)
                        m = segment_max(s, k)
                    differences(s, m)
                    dve.wait_ge(a_st[b], jb + 1)

                loop_start()
                logits(0, 0)
                need(ring_copy(0, 0))
                for k in range(G):
                    need(running_max(0, k))
                messages(0)
                for k in range(G - 2, -1, -1):
                    last = segment_max(0, k)
                    need(last)
                differences(0, last)
                step(0, 1, False, 0, False)
                with dve.Fori(1, AHALF) as j:
                    loop_start()
                    step(j, 0, True, j - 1, True)
                    step(j, 1, True, j, True)
                loop_start()
                weighted(AHALF - 1, 1)
                need(rescaled(1))
                slot_free(AHALF - 1, 1, True)
                store_index(AHALF - 1, 1)
                need(running_sum(1, 0))
                for k in range(1, G - 1):
                    need(mark(running_sum(1, k)))
                running_sum(1, G - 1).then_inc(a_st[1], 1)
                dve.wait_ge(a_st[1], AHALF)

                for half in range(2):
                    link(v.memset(tT[:, 4 + half, 0:1], -BIG))
                v.memset(tT[:, 0:4, 0:1], 0.0).then_inc(s_tail, 1)
                dve.wait_ge(s_turn, 2)
                link(v.tensor_copy(tT[:, 0:4, 1:P], ps[:, 0, :].rearrange("p (c q) -> p c q", q=P)[:, :, 0:P - 1]))
                for half in range(2):
                    m, c = tT[:, 4 + half, :], cT[:, 4 + half, :]
                    link(tt(m[:, 1:P], ps[:, 1, half * P:half * P + P - 1], rows[:, CONT_NEG, 1:P], ALU.add))
                    link(v.tensor_tensor_scan(c, rows[:, BOTH_NEG, :], m, 0.0, ALU.add, ALU.max))
                    link(v.memset(ab[:, half, 0, 0:1], 0.0))
                    link(tt(ab[:, half, 0, 1:P], rows[:, BOTH_NEG, 1:P], c[:, 0:P - 1], ALU.add))
                    link(tt(ab[:, half, 0, 1:P], ab[:, half, 0, 1:P], c[:, 1:P], ALU.subtract))
                    last = tt(ab[:, half, 1, :], m, c, ALU.subtract)
                    if half == 0:
                        link(last)
                ask(last)
                for t in range(4):
                    link(tt(tT[:, t, :], tT[:, t, :], ab[:, t % 2, 1, :], ALU.mult))
                    last = v.tensor_tensor_scan(cT[:, t, :], ab[:, t % 2, 0, :], tT[:, t, :], 0.0, ALU.mult, ALU.add)
                last.then_inc(s_car, 1)
                dve.wait_ge(s_back, 2)
                dve.wait_ge(s_fixed, 16 * 3)
                mine, done, w = st[:, 0, 0, :], st[:, 0, 1, :], bbuf[:, 0, 0]
                theirs = stt[:].rearrange("p t c -> p (t c)")
                link(tt(done[:, 2 * DD:TW], mine[:, 2 * DD:TW], ps[:, 3, 0:DD], ALU.max))
                link(tt(w[:, 0, :], mine[:, 2 * DD:TW], done[:, 2 * DD:TW], ALU.subtract))
                ask(tt(w[:, 1, :], ps[:, 3, 0:DD], done[:, 2 * DD:TW], ALU.subtract))
                for t in range(2):
                    part = slice(t * DD, (t + 1) * DD)
                    link(tt(theirs[:, part], ps[:, 2, part], w[:, 1, :], ALU.mult))
                    link(tt(done[:, part], mine[:, part], w[:, 0, :], ALU.mult))
                link(tt(done[:, 0:2 * DD], done[:, 0:2 * DD], theirs, ALU.add))
                link(v.memset(nt[:, 0:1, :], 0.0))
                v.memset(nt[:, 0:1, :], 0.0).then_inc(s_lead, 1)

                for c in range(NCH):
                    dve.wait_ge(s_att[c % 2], 16 * (c // 2 + 1))
                    b = bbuf[:, c % 2, 0:DC]
                    link(v.tensor_scalar(b[:, :, 0, :], b[:, :, 0, :], TINY, None, ALU.max))
                    link(v.reciprocal(b[:, :, 0, :], b[:, :, 0, :]))
                    tt(dbuf[:, 0, 0:DC, :], b[:, :, 1, :], b[:, :, 0, :], ALU.mult).then_inc(s_attu, 1)
                    dve.wait_ge(s_attu, c + 1)
                    link(v.tensor_reduce(got[:, c * DC:(c + 1) * DC, :], dbuf[:, 0, 0:DC, :].rearrange("p b (i o) -> p b o i", o=D), AX.X, ALU.add))

            products = [0]

            def dense(dest, ins, b, relu):
                ins.then_inc(s_din, 1)
                products[0] += 1
                dve.wait_ge(s_dmm, products[0])
                for half, (lo, hi) in enumerate(((0, PB * DC), (PB * DC, NB))):
                    link(tt(dest[:, lo:hi, :], ps[:, 2 + half, 0:(hi - lo) * D].rearrange("p (b c) -> p b c", c=D),
                            bias[:, b, :].unsqueeze(1).to_broadcast([P, hi - lo, D]), ALU.add))
                if relu:
                    link(v.tensor_scalar(dest[:], dest[:], 0.0, None, ALU.max))

            narrow_pass(0)
            link(tt(got[:], got[:], wide(full[:]), ALU.mult))
            link(tt(got[:], got[:], x0[:], ALU.add))
            layer_norm(xa, got).then_inc(s_feat, 1)
            attention()
            link(tt(got[:], got[:], xa[:], ALU.add))
            layer_norm(xb, got).then_inc(s_feat, 1)
            dve.wait_ge(s_feat, 2)
            split(xb)
            narrow_pass(1)
            dense(got, tt(nt[:], got[:], wide(full[:]), ALU.mult), 0, False)
            link(tt(got[:], got[:], xb[:], ALU.add))
            link(layer_norm(xa, got))
            link(v.tensor_scalar(bad[:], full[:], -POISON, POISON, ALU.mult, ALU.add))
            link(tt(xa[:], xa[:], wide(full[:]), ALU.mult))
            tt(xa[:], xa[:], wide(bad[:]), ALU.add).then_inc(s_feat, 1)
            dve.wait_ge(s_feat, 3)
            split(xa)
            for i, (own, dest) in enumerate(((xa, xb), (xb, got))):
                narrow_pass(2 + i)
                link(tt(nu[:], got[:], wide(full[:]), ALU.mult))
                link(tt(nt[:], nu[:], own[:], ALU.add))
                link(v.tensor_scalar(bad[:], nt[:, :, 0], POISON * 0.5, None, ALU.is_gt))
                link(v.tensor_scalar(st1[:], bad[:], -1.0, 1.0, ALU.mult, ALU.add))
                link(v.scalar_tensor_tensor(nt[:], own[:], epsb[:, i:i + 1], nt[:], ALU.mult, ALU.add))
                dense(got, tt(nt[:], nt[:], wide(st1[:]), ALU.mult), 1 + 2 * i, True)
                dense(dest, v.tensor_copy(nt[:], got[:]), 2 + 2 * i, i == 0)
                if i == 0:
                    link(tt(dest[:], dest[:], wide(st1[:]), ALU.mult))
                    link(v.tensor_scalar(st2[:], bad[:], POISON, None, ALU.mult))
                    tt(dest[:], dest[:], wide(st2[:]), ALU.add).then_inc(s_feat, 1)
                    dve.wait_ge(s_feat, 4)
                    split(xb)
            link(v.tensor_reduce(st1[:], got[:], AX.X, ALU.max))
            ask(tt(nt[:], got[:], wide(st1[:]), ALU.subtract))
            ask(v.tensor_reduce(st1[:], nu[:], AX.X, ALU.add))
            link(tt(nt[:], nt[:], wide(st2[:]), ALU.subtract))
            link(v.tensor_scalar(st1[:], bad[:], -1.0, 1.0, ALU.mult, ALU.add))
            link(tt(xa[:], xa[:], wide(st1[:]), ALU.mult))
            link(tt(got[:], nt[:], xa[:], ALU.add))
            link(layer_norm(got, got))
            link(v.tensor_scalar(bad[:], bad[:], BIG, BIG, ALU.mult, ALU.mult))
            link(tt(bad[:], bad[:], bad[:], ALU.subtract))
            tt(nt[:], got[:], wide(bad[:]), ALU.add).then_inc(s_feat, 1)


def kernel(x, src, dst, edge_attr_16, edge_weight, edge_weight1, L1_gnn_W_msg, L1_gnn_b_msg, L1_gnn_W_attn,
           L1_gnn_b_attn, L2_gnn_W, L2_gnn_b, L3_gnn_eps1, L3_gnn_w1a, L3_gnn_b1a, L3_gnn_w1b, L3_gnn_b1b,
           L3_gnn_eps2, L3_gnn_w2a, L3_gnn_b2a, L3_gnn_w2b, L3_gnn_b2b):
    import numpy as np
    import concourse.bacc as bacc
    from concourse.bass_utils import run_bass_kernel_spmd as run

    def padded(a, rows, fill=0):
        a = np.asarray(a)
        return np.concatenate([a, np.full((rows - a.shape[0],) + a.shape[1:], fill, a.dtype)])

    d = np.asarray(dst)
    arrays = {
        "x": padded(x, NN),
        "src": padded(src, P * K).reshape(P, K),
        "dst": np.concatenate([np.full((1, K), -1, d.dtype), padded(d, P * K, N).reshape(P, K), np.full((1, K), N + 1, d.dtype)]),
        "ew": padded(edge_weight, P * K).reshape(P, K),
        "ew1": padded(edge_weight1, P * K).reshape(P, K),
        "ef": padded(edge_attr_16, P * K).reshape(P, K * D),
        "wpad": np.concatenate([
            np.concatenate([np.asarray(L1_gnn_W_attn), np.asarray(L1_gnn_W_msg)], 1),
            np.concatenate([np.asarray(L1_gnn_b_attn), np.asarray(L1_gnn_b_msg)])[None]]),
        "ident": np.eye(P, dtype=np.float32),
        "dense_w": np.stack([np.asarray(L2_gnn_W).T] + [np.asarray(w) for w in (L3_gnn_w1a, L3_gnn_w1b, L3_gnn_w2a, L3_gnn_w2b)]),
        "biases": np.stack([np.asarray(b) for b in (L2_gnn_b, L3_gnn_b1a, L3_gnn_b1b, L3_gnn_b2a, L3_gnn_b2b)]),
        "eps": np.stack([np.asarray(L3_gnn_eps1), np.asarray(L3_gnn_eps2)]),
    }
    arrays = {k: np.ascontiguousarray(v) for k, v in arrays.items()}
    nc = bacc.Bacc("TRN2", target_bir_lowering=False, num_devices=1)
    args = [nc.dram_tensor(f"in_{k}", v.shape, mybir.dt.from_np(v.dtype), kind="ExternalInput").ap() for k, v in arrays.items()]
    out = nc.dram_tensor("out", (NN, D), FP, kind="ExternalOutput").ap()
    gnn_program(nc, *args, out)
    result = run(nc, [{f"in_{k}": v for k, v in arrays.items()}], core_ids=[0])
    return result.results[0]["out"][:N]
```

```python
import concourse.bass as bass
from concourse import mybir
from contextlib import ExitStack

P = 128
N, E, D = 6250, 200000, 16
U = 28
R = 14
A = U - R
G = 7
K = -(-E // (P * 2 * U)) * 2 * U
NB = -(-(N + 1) // P)
NN = P * NB
NG = K // U
AG = K // G
DD = D * D
TW = 3 * DD
BIG = 1e38
OOB = float(1 << 20)
POISON = 1e30
TINY = 1e-30
EPS = 1e-5
DC = 7
Q = 7
QW = Q * D
DW = DC * D
NCH = NB // DC
PB = 4
F = D + 1
FROM = (0, 6, 10)
NEW = (0, 6, 12, D)
CF = 6
CW = CF * F
HG = 4
assert NB % 2 == 1 and NB // 2 + 1 < NG // 2 and NB % DC == 0 and K % (2 * G) == 0 and NG >= NB and G * D == DW
CONT, BOTH, CONT_NEG, BOTH_NEG = range(4)

assert NB == Q * Q and PB * QW <= 512 and R <= 4 * PB and K % DW == 0

FP = mybir.dt.float32
BF = mybir.dt.bfloat16
HF = mybir.dt.float16
I32 = mybir.dt.int32
ALU = mybir.AluOpType
ACT = mybir.ActivationFunctionType
AX = mybir.AxisListType


def gnn_program(nc, x, src_in, dst_in, ew_in, ew1_in, ef_in, att_w, ident, dense_w, biases, eps, out):
    es = ExitStack()

    def sb(name, shape, dt=FP):
        return es.enter_context(nc.sbuf_tensor(name, shape, dt))

    def sem(name):
        return es.enter_context(nc.semaphore(name))

    def ring(name):
        return [sem(f"{name}_{i}") for i in range(2)]

    def dram(name, shape):
        return nc.dram_tensor(name, shape, FP).ap()

    with es:
        feat = [x] + [dram(f"feat{i}", (NN, D)) for i in range(1, 5)]
        run_tab = [dram(f"run_tab{i}", (P * K, D)) for i in range(4)]
        att_tab = dram("att_tab", (NN, TW))
        quot_tab = nc.dram_tensor("quot_tab", (K, P), HF).ap()

        src = nc.dram_tensor("src_sorted", (P, K), I32).ap()
        dst = nc.dram_tensor("dst_sorted", (P + 2, K), I32).ap()
        ew, ew1, ef = dram("ew_sorted", (P, K)), dram("ew1_sorted", (P, K)), dram("ef_sorted", (P, K * F))
        place_tab = dram("place_tab", (NN, 1))

        idm = sb("idm", [P, P])
        ones = sb("ones", [P, P])
        edgei = sb("edgei", [P, 3], I32)
        edgef = sb("edgef", [P, 3])
        resets = sb("resets", [P, 2, K])
        neg, keep = resets[:, 0, :], resets[:, 1, :]
        scat = sb("scat", [P, K])
        nidi = sb("nidi", [P, NG + 1], I32)
        nid = sb("nid", [P, NG + 1])
        pidx = sb("pidx", [P, NG])
        cle = sb("cle", [P, NG])
        clt = sb("clt", [P, NG])
        full = sb("full", [P, NB])
        endf = sb("endf", [P, NB])
        endi = sb("endi", [P, NB], I32)
        counti = sb("counti", [P, 2, Q], I32)
        count = sb("count", [P, 2, Q])
        rem = sb("rem", [P, K], BF)
        fcol = sb("fcol", [P, 5])
        fidx = sb("fidx", [P, 3], I32)
        diag = sb("diag", [P, 3, P])
        frow = sb("frow", [P, P])
        rows = sb("rows", [P, 4, P])

        flag = sb("flag", [P, 1], I32)
        place = sb("place", [P, NB])
        below = sb("below", [P, NB])
        lower = sb("lower", [P, P])
        loweri = sb("loweri", [P, P], I32)
        key = sb("key", [P, 2], I32)
        rec = sb("rec", [P, 2 + F])
        got_place = sb("got_place", [P, 1])
        tcol = sb("tcol", [P, 6])
        spot = sb("spot", [P, 3], I32)

        sidx = sb("sidx", [P, 2, U], I32)
        wts = sb("wts", [P, 2, U])
        msg = sb("msg", [P, 2, U, D])
        val = sb("val", [P, 2, U, D])
        run = sb("run", [P, 2, U, D])
        mring = sb("mring", [P, 2, U])
        pring = sb("pring", [P, 2], I32)
        parts = sb("parts", [P, NB, 3, D], BF)
        amask = sb("amask", [P, R, Q])
        tailT = sb("tailT", [D, P])
        carryT = sb("carryT", [D, P])
        lead = sb("lead", [P, D])
        lead2 = sb("lead2", [P, D])

        aidx = sb("aidx", [P, 2, G], I32)
        efs = sb("efs", [P, 2, G * F])
        hsrc = sb("hsrc", [P, 2, G, D])
        z = sb("z", [P, 2, G, D * F])
        zT = sb("zT", [P, 2, 3 * P])
        wsb = sb("wsb", [P, 3, CF * 2 * D])
        aring = sb("aring", [P, 2, 2, G])
        scidx = sb("scidx", [P, 2, G], I32)
        dbuf = sb("dbuf", [P, 2, G + 1, DD])
        wide_buf = sb("wide_buf", [P, (G + 1) * 2 * DD + 2 * G * DD])
        bbuf = wide_buf[:, 0:(G + 1) * 2 * DD].rearrange("p (g t c) -> p g t c", t=2, c=DD)
        mbuf = wide_buf[:, (G + 1) * 2 * DD:].rearrange("p (a g c) -> p a g c", a=2, c=DD)
        amax = sb("amax", [P, 2, G, DD])
        smax = sb("smax", [P, G - 1, DD])
        st = sb("st", [P, 2, G, TW])
        stt = sb("stt", [P, 2, DD])
        ab = sb("ab", [P, 2, 2, P])
        slices = amax[:].rearrange("p a g c -> p (a g c)")[:, 0:2 * K].rearrange("p (a k) -> p a k", a=2).bitcast(I32)
        dsti = slices[:, 0, :]
        dstf = wide_buf[:, 0:K + 2]
        srci = slices[:, 1, :]
        raw = dbuf[:].rearrange("p a g c -> p (a g c)")
        quot = raw[:, 0:R * P].bitcast(HF)[:, 0:2 * R * P].rearrange("p (a e) -> p a e", a=2)
        picked = raw[:, R * P:R * P + R * QW].rearrange("p (r q c) -> p r q c", q=Q, c=D)
        quotT = raw[:, 0:(K // DW) * P // 2].bitcast(HF).rearrange("p (c q) -> p c q", q=P)
        flat = st[:].rearrange("p a g c -> p (a g c)")
        hot = [t[:, 0:Q * R * P // 2].bitcast(BF).rearrange("p (m e) -> p m e", m=Q)
               for t in (wide_buf, flat)]
        junk = flat[:, Q * R * P // 2:Q * R * P // 2 + K]
        quotf = flat[:, 0:K]
        quot_src = flat[:, K:2 * K]
        compared = flat[:, 0:NG * P].rearrange("p (b q) -> p b q", b=NG)

        SW = DC * 2 * DD
        nodes = [t.rearrange("p (b t c) -> p b t c", t=2, c=DD) for t in
                 [wide_buf[:, i * SW:(i + 1) * SW] for i in range(2)] + [flat[:, i * SW:(i + 1) * SW] for i in range(3)]
                 + [z[:].rearrange("p a g c -> p (a g c)")[:, 0:SW]]]

        x0 = sb("x0", [P, NB, D])
        xa = sb("xa", [P, NB, D])
        xb = sb("xb", [P, NB, D])
        got = sb("got", [P, NB, D])
        nt = sb("nt", [P, NB, D])
        nu = sb("nu", [P, NB, D])
        zt = got[:].rearrange("p b c -> p (b c)")[:, 0:TW]
        tT = nt[:].rearrange("p b c -> p (b c)")[:, 0:6 * P].rearrange("p (t q) -> p t q", q=P)
        cT = nu[:].rearrange("p b c -> p (b c)")[:, 0:6 * P].rearrange("p (t q) -> p t q", q=P)
        vT = sb("vT", [P, NCH, P])
        bd = sb("bd", [P, 5, DW])
        bias = sb("bias", [P, 5, D])
        epsb = sb("epsb", [P, 2])
        st1 = sb("st1", [P, NB])
        st2 = sb("st2", [P, NB])
        st3 = sb("st3", [P, NB])
        bad = sb("bad", [P, NB])

        ps = es.enter_context(nc.psum_tensor("ps", [P, 8, 512], FP))

        s_list = sem("s_list")
        s_const = sem("s_const")
        s_zero = sem("s_zero")
        s_copy = sem("s_copy")
        s_part = sem("s_part")
        s_total = sem("s_total")
        s_flag = sem("s_flag")
        q_row = sem("q_row")
        q_rowu = sem("q_rowu")
        q_place = sem("q_place")
        q_placed = sem("q_placed")
        q_chain = sem("q_chain")
        q_raw = sem("q_raw")
        q_load = sem("q_load")
        q_diag = sem("q_diag")
        q_all = sem("q_all")
        q_got = sem("q_got")
        q_spot = sem("q_spot")
        q_put = [sem(f"q_put{i}") for i in range(3)]
        q_done = sem("q_done")
        q_again = sem("q_again")
        s_quot = sem("s_quot")
        s_quots = sem("s_quots")
        s_parts = sem("s_parts")
        s_w = sem("s_w")
        s_tab = sem("s_tab")
        s_iota = sem("s_iota")
        s_chain = sem("s_chain")
        s_loop = sem("s_loop")
        s_diag = sem("s_diag")
        s_rows = sem("s_rows")
        s_pidx = ring("s_pidx")
        s_slice = ring("s_slice")
        s_pool = sem("s_pool")
        s_sp = sem("s_sp")
        s_idxr = sem("s_idxr")
        s_fixed = sem("s_fixed")
        s_node = [sem(f"s_node{i}") for i in range(4)]
        s_tail = sem("s_tail")
        s_turn = sem("s_turn")
        s_car = sem("s_car")
        s_back = sem("s_back")
        s_lead = sem("s_lead")
        s_att = [sem(f"s_att{i}") for i in range(NCH)]
        s_attu = sem("s_attu")
        s_feat = sem("s_feat")
        s_feats = sem("s_feats")
        s_din = sem("s_din")
        s_dtr = sem("s_dtr")
        s_dcp = sem("s_dcp")
        s_dmm = sem("s_dmm")
        s_asked = sem("s_asked")
        s_acted = sem("s_acted")
        s_ln = sem("s_ln")
        s_out = sem("s_out")
        NARROW = ("idx", "w", "quot", "hot", "pick", "read", "got", "mul", "act", "run", "put")
        narrow = {k: ring(f"n_{k}") for k in NARROW}
        a_idx = ring("a_idx")
        a_ef = ring("a_ef")
        a_got = ring("a_got")
        a_z = ring("a_z")
        a_tr = ring("a_tr")
        a_trs = ring("a_trs")
        a_mm = ring("a_mm")
        a_out = ring("a_out")
        a_d = ring("a_d")
        a_exp = ring("a_exp")
        a_w = ring("a_w")
        a_max = ring("a_max")
        a_st = ring("a_st")
        a_sc = ring("a_sc")

        ZEROS = NB // 2
        HALF = NG // 2
        AHALF = AG // 2
        block = es.enter_context(nc.Block())

        @block.sync
        def _(sp):
            def narrow_pass(n):
                q, done = narrow, n * HALF
                table = run_tab[n].rearrange("(p k) c -> p (k c)", p=P)

                def load(g, s):
                    sp.dma_start(sidx[:, s, :], src[:, bass.ds(g * U, U)]).then_inc(q["idx"][s], 16)
                    if n < 2:
                        sp.dma_start(wts[:, s, :], (ew, ew1)[n][:, bass.ds(g * U, U)]).then_inc(q["w"][s], 16)

                def load_quot(g, s):
                    sp.dma_start(quot[:, s, :], quot_tab.rearrange("k q -> (k q)")[bass.ds((g * U + A) * P, R * P)]
                                 .partition_broadcast(P)).then_inc(q["quot"][s], 16)

                def round_(j, more, more_quot):
                    for s in range(2):
                        sp.wait_ge(q["run"][s], done + j + 1)
                        sp.sem_inc(s_sp, 1)
                        sp.dma_start(table[:, bass.ds((2 * j + s) * (U * D), U * D)],
                                     run[:, s].rearrange("p u c -> p (u c)")).then_inc(q["put"][s], 16)
                        if more:
                            load(2 * j + 2 + s, s)
                        if more_quot or (more and s == 0):
                            sp.wait_ge(q["hot"][1 - s], done + j + 1 + s)
                            sp.sem_inc(s_sp, 1)
                            load_quot(2 * j + 3 + s, 1 - s)

                for s in range(2):
                    load(s, s)
                if n == 0:
                    sp.wait_ge(s_quots, 16)
                for s in range(2):
                    load_quot(s, s)
                sp.wait_ge(q["hot"][0], done + 1)
                load_quot(2, 0)
                with sp.Fori(0, HALF - 2) as j:
                    round_(j, True, True)
                round_(HALF - 2, True, False)
                round_(HALF - 1, False, False)

            def put_feat(i, tile):
                sp.wait_ge(s_feat, i)
                sp.dma_start(feat[i].rearrange("(p b) c -> p (b c)", p=P),
                             tile[:].rearrange("p b c -> p (b c)")).then_inc(s_feats, 16)

            def attention_loads(features):
                def load(g, s):
                    sp.dma_start(aidx[:, s, :], src[:, bass.ds(g * G, G)]).then_inc(a_idx[s], 16)
                    sp.dma_start(efs[:, s, :], features[:, bass.ds(g * (G * F), G * F)]).then_inc(a_ef[s], 16)

                for s in range(2):
                    load(s, s)
                with sp.Fori(0, AHALF - 1) as j:
                    for s in range(2):
                        sp.wait_ge(a_z[s], j + 1)
                        sp.sem_inc(s_sp, 1)
                        load(2 * j + 2 + s, s)

            def attention_states():
                states = att_tab.rearrange("(p b) c -> p b c", p=P)
                sp.wait_ge(s_fixed, 16 * 4)
                for c in range(NCH):
                    if c >= len(nodes):
                        sp.wait_ge(s_attu, c - len(nodes) + 1)
                    sp.dma_start(nodes[c % len(nodes)].rearrange("p b t c -> p b (t c)"),
                                 states[:, c * DC:(c + 1) * DC, 0:2 * DD]).then_inc(s_att[c], 16)

            def sort():
                with sp.Fori(1, P + 1) as r:
                    sp.dma_start(srci, dst_in[bass.ds(r, 1), :].rearrange("a k -> (a k)").partition_broadcast(P)).then_inc(q_row, 16)
                    sp.wait_ge(q_rowu, r)
                    sp.sem_inc(s_sp, 1)
                sp.wait_ge(q_place, 2)
                sp.dma_start(place_tab.rearrange("(p b) c -> p (b c)", p=P), place[:]).then_inc(q_placed, 16)
                with sp.Fori(0, K) as k:
                    with nc.allow_non_contiguous_dma(reason="one edge of each slice"):
                        for dest, source in ((key[:, 0:1], dst_in[1:P + 1, bass.ds(k, 1)]), (key[:, 1:2], src_in[:, bass.ds(k, 1)]),
                                             (rec[:, 0:1], ew_in[:, bass.ds(k, 1)]), (rec[:, 1:2], ew1_in[:, bass.ds(k, 1)]),
                                             (rec[:, 2:2 + F], ef_in[:, bass.ds(k * F, F)])):
                            sp.dma_start(dest, source).then_inc(q_raw, 16)
                    sp.wait_ge(q_raw, 16 * 5)
                    sp.sem_clear(q_raw)
                    sp.sem_inc(q_load, 1)
                    sp.wait_ge(q_done, k + 1)
                    sp.sem_inc(s_sp, 1)

            for dest, source in ((src, src_in), (ew, ew_in), (dst, dst_in), (ew1, ew1_in)):
                sp.dma_start(dest, source).then_inc(s_copy, 16)
            sp.wait_ge(s_copy, 16 * 4)
            sp.wait_ge(s_flag, 1)
            unsorted = sp.value_load(flag[0:1, 0:1], min_val=0, max_val=P * K)
            with sp.If(unsorted > 0):
                sort()
            sp.end_ifs()
            narrow_pass(0)
            put_feat(1, xa)
            with sp.If(unsorted > 0):
                attention_loads(ef)
            with sp.Else():
                attention_loads(ef_in)
            sp.end_ifs()
            attention_states()
            put_feat(2, xb)
            narrow_pass(1)
            put_feat(3, xa)
            narrow_pass(2)
            put_feat(4, xb)
            narrow_pass(3)
            sp.wait_ge(s_feat, 5)
            sp.dma_start(out.rearrange("(p b) c -> p (b c)", p=P),
                         nt[:].rearrange("p b c -> p (b c)")).then_inc(s_out, 16)
            sp.wait_ge(s_out, 16)

        @block.gpsimd
        def _(pool):
            def rows_at(ap):
                return bass.IndirectOffsetOnAxis(ap=ap, axis=0)

            def gather(dest, table, idx):
                return pool.indirect_dma_start(dest, None, table, rows_at(idx))

            def scatter(table, idx, source, **kw):
                return pool.indirect_dma_start(table, rows_at(idx), source, None, **kw)

            def narrow_pass(n, table):
                q, done = narrow, n * HALF
                used = q["mul"] if n < 2 else q["run"]

                def round_(j, first):
                    for s in range(2):
                        pool.wait_ge(q["idx"][s], 16 * (done + j + 1))
                        if not first:
                            pool.wait_ge(used[s], done + j)
                        pool.sem_inc(s_pool, 1)
                        for u in range(A):
                            gather(msg[:, s, u, :], table, sidx[:, s, u:u + 1]).then_inc(q["got"][s], 16)
                        if n == 0:
                            pool.wait_ge(s_pidx[s], j + 1)
                            pool.sem_inc(s_pool, 1)
                            gather(slices[:, s, :], dst, pring[:, s:s + 1]).then_inc(s_slice[s], 16)

                if n == 0:
                    round_(0, True)
                with pool.Fori(1 if n == 0 else 0, HALF) as j:
                    round_(j, False)
                if n == 0:
                    pool.wait_ge(s_idxr, 1)
                for s in range(2):
                    pool.wait_ge(q["put"][s], 16 * (done + HALF))
                fixes = 2 * n if n == 0 else 2 * n + 2
                gather(lead[:], run_tab[n], fidx[:, 0:1]).then_inc(s_fixed, 16)
                pool.wait_ge(s_lead, fixes // 2 + 1)
                scatter(run_tab[n], fidx[:, 0:1], lead2[:]).then_inc(s_fixed, 16)
                pool.wait_ge(s_fixed, 16 * (fixes + 2))
                if n == 0:
                    pool.wait_ge(s_tab, 16 * (ZEROS + 1))
                for b in range(NB):
                    gather(got[:, b, :], run_tab[n], endi[:, b:b + 1]).then_inc(s_node[n], 16)

            def attention():
                def fetch(j, s, first):
                    pool.wait_ge(a_idx[s], 16 * (j + 1))
                    if not first:
                        pool.wait_ge(a_z[s], j)
                    pool.sem_inc(s_pool, 1)
                    for k in range(G):
                        gather(hsrc[:, s, k, :], feat[1], aidx[:, s, k:k + 1]).then_inc(a_got[s], 16)

                def put(j, s):
                    pool.wait_ge(a_st[s], j + 1)
                    pool.sem_inc(s_pool, 1)
                    for k in range(G):
                        scatter(att_tab, scidx[:, s, k:k + 1], st[:, s, k, :],
                                bounds_check=NN - 1, oob_is_err=False).then_inc(a_sc[s], 16)

                pool.wait_ge(s_tab, 16 * (ZEROS + 1))
                for g in range(4):
                    fetch(g // 2, g % 2, g < 2)
                with pool.Fori(2, AHALF) as j:
                    for s in range(2):
                        fetch(j, s, False)
                        put(j - 2, s)
                for g in range(4):
                    put(AHALF - 2 + g // 2, g % 2)
                for s in range(2):
                    pool.wait_ge(a_sc[s], 16 * G * AHALF)
                pool.wait_ge(s_tail, 2)
                gather(st[:, 0, 0, :], att_tab, fidx[:, 1:2]).then_inc(s_fixed, 16)
                pool.wait_ge(s_lead, 2)
                scatter(att_tab, fidx[:, 2:3], st[:, 0, 1, :],
                        bounds_check=NN - 1, oob_is_err=False).then_inc(s_fixed, 16)

            def one(table):
                return table.rearrange("p (k c) -> (p k) c", c=1)

            def sort():
                pool.iota(loweri[:], [[1, P]], base=0, channel_multiplier=-1).then_inc(q_place, 1)
                pool.wait_ge(q_placed, 16)
                with pool.Fori(0, K) as k:
                    pool.wait_ge(q_load, k + 1)
                    pool.sem_inc(s_pool, 1)
                    gather(got_place[:], place_tab, key[:, 0:1]).then_inc(q_got, 16)
                    pool.wait_ge(q_spot, k + 1)
                    pool.sem_inc(s_pool, 1)
                    scatter(one(src), spot[:, 0:1], key[:, 1:2]).then_inc(q_put[0], 16)
                    scatter(one(dst), spot[:, 1:2], key[:, 0:1]).then_inc(q_put[0], 16)
                    scatter(one(ew), spot[:, 0:1], rec[:, 0:1]).then_inc(q_put[1], 16)
                    scatter(one(ew1), spot[:, 0:1], rec[:, 1:2]).then_inc(q_put[1], 16)
                    scatter(ef.rearrange("p (k c) -> (p k) c", c=F), spot[:, 0:1], rec[:, 2:2 + F]).then_inc(q_put[2], 16)
                    scatter(place_tab, spot[:, 2:3], tcol[:, 3:4], bounds_check=NN - 1, oob_is_err=False).then_inc(q_put[2], 16)
                    for i in range(3):
                        pool.wait_ge(q_put[i], k * 32 + 32)
                        pool.sem_inc(s_pool, 1)
                    pool.sem_inc(q_done, 1)

            pool.memset(bd[:], 0.0).then_inc(s_zero, 1)
            pool.memset(wsb[:], 0.0).then_inc(s_zero, 1)
            pool.memset(zt, 0.0).then_inc(s_zero, 1)
            pool.memset(ones[:], 1.0).then_inc(s_zero, 1)
            pool.iota(nidi[:, 0:NG], [[1, NG]], base=0, channel_multiplier=NB).then_inc(s_iota, 1)
            pool.iota(nidi[:, NG:NG + 1], [[0, 1]], base=-1, channel_multiplier=K).then_inc(s_iota, 1)
            pool.iota(counti[:, 0, :], [[1, Q]], base=0, channel_multiplier=Q).then_inc(s_iota, 1)
            pool.iota(counti[:, 1, :], [[1, Q]], base=0, channel_multiplier=0).then_inc(s_iota, 1)
            pool.wait_ge(s_copy, 16 * 4)
            pool.wait_ge(s_flag, 1)
            unsorted = pool.value_load(flag[0:1, 0:1], min_val=0, max_val=P * K)
            with pool.If(unsorted > 0):
                sort()
            pool.end_ifs()
            narrow_pass(0, feat[0])
            pool.wait_ge(s_feats, 16)
            attention()
            for n in range(1, 4):
                pool.wait_ge(s_feats, 16 * (n + 1))
                narrow_pass(n, feat[n + 1])

        @block.scalar
        def _(act):
            acted = [0]

            def asked(dest, source, func):
                acted[0] += 1
                act.wait_ge(s_asked, acted[0])
                nc.scalar.activation(dest, source, func).then_inc(s_acted, 1)

            def dense(i):
                act.wait_ge(s_dtr, i + 1)
                nc.scalar.activation(vT[0:DW, 0:PB, :], ps[0:DW, 0, 0:PB * P].rearrange("p (c q) -> p c q", q=P), ACT.Copy)
                nc.scalar.activation(vT[0:DW, PB:NCH, :], ps[0:DW, 1, 0:(NCH - PB) * P].rearrange("p (c q) -> p c q", q=P),
                                     ACT.Copy).then_inc(s_dcp, 1)

            def load_lists(src, dst, signal):
                act.dma_start(dsti, dst[1:P + 1, :]).then_inc(signal, 16)
                for c, (r, k) in enumerate(((0, K - 1), (0, 0), (2, 0))):
                    act.dma_start(edgei[:, c:c + 1], dst[r:r + P, k:k + 1], allow_slow_non_contiguous=True).then_inc(signal, 16)
                act.dma_start(srci, src).then_inc(signal, 16)

            load_lists(src_in, dst_in, s_list)
            act.dma_start(idm[:], ident).then_inc(s_const, 16)
            act.dma_start(x0[:].rearrange("p b c -> p (b c)"), x.rearrange("(p b) c -> p (b c)", p=P)).then_inc(s_const, 16)
            for i in range(2):
                act.dma_start(epsb[:, i:i + 1], eps[i:i + 1].partition_broadcast(P)).then_inc(s_const, 16)
            for i in range(5):
                act.dma_start(bias[:, i, :], biases[i].partition_broadcast(P)).then_inc(s_const, 16)
            act.wait_ge(s_copy, 16 * 4)
            act.wait_ge(s_flag, 1)
            unsorted = act.value_load(flag[0:1, 0:1], min_val=0, max_val=P * K)
            with act.If(unsorted > 0):
                act.wait_ge(q_done, K)
                load_lists(src, dst, q_again)
            act.end_ifs()
            act.wait_ge(s_quot, 3)
            act.dma_start(quot_tab.rearrange("(c r) q -> r c q", r=DW), quotT[0:DW]).then_inc(s_quots, 16)
            act.wait_ge(s_zero, 3)
            for i in range(5):
                for c in range(DC):
                    act.dma_start(bd[c * D:(c + 1) * D, i, c * D:(c + 1) * D], dense_w[i]).then_inc(s_w, 16)
            for i in range(D):
                c = sum(i >= start for start in NEW[1:3])
                act.dma_start(wsb[(i - FROM[c]) * F:(i - FROM[c] + 1) * F, c, (i - NEW[c]) * 2 * D:(i - NEW[c] + 1) * 2 * D],
                              att_w[:, i * 2 * D:(i + 1) * 2 * D]).then_inc(s_w, 16)
            q = narrow

            def tanh_round(j):
                for s in range(2):
                    act.wait_ge(q["mul"][s], j + 1)
                    nc.scalar.activation(val[:, s], val[:, s], ACT.Tanh).then_inc(q["act"][s], 1)

            def zero_states(first, blocks):
                act.dma_start(att_tab.rearrange("(p b) c -> p b c", p=P)[:, bass.ds(first, blocks), :],
                              zt.unsqueeze(1).to_broadcast([P, blocks, TW])).then_inc(s_tab, 16)

            tanh_round(0)
            zero_states(0, 1)
            with act.Fori(1, ZEROS + 1) as j:
                tanh_round(j)
                zero_states(j * 2 - 1, 2)
            with act.Fori(ZEROS + 1, HALF) as j:
                tanh_round(j)
            asked(st3[:], st2[:], ACT.Sqrt)

            def copy_out(s, which, dest, lo, hi):
                return nc.scalar.activation(
                    dest[:, s, lo:hi, :].rearrange("p g (i o) -> p g i o", o=D),
                    ps[:, lo:hi, :].rearrange("p g (i t o) -> p g i t o", t=2, o=D)[:, :, :, which, :], ACT.Copy)

            def products(j, s, first):
                for k in range(G):
                    act.wait_ge(a_tr[s], j * G + k + 1)
                    nc.scalar.activation(zT[0:CW, (s * G + k) % 2, :], ps[0:CW, G, 0:3 * P], ACT.Copy).then_inc(a_trs[s], 1)
                    if k == HG:
                        act.wait_ge(a_mm[s], j * 2 + 1)
                        copy_out(s, 0, dbuf, 0, HG)
                    if k == HG + 1 and not first:
                        act.wait_ge(a_w[s], j)
                    if k == HG + 1:
                        copy_out(s, 1, mbuf, 0, HG).then_inc(a_out[s], 1)
                act.wait_ge(a_mm[s], j * 2 + 2)
                copy_out(s, 0, dbuf, HG, G)
                copy_out(s, 1, mbuf, HG, G).then_inc(a_out[s], 1)

            def weights(j, s, first):
                act.wait_ge(a_d[s], j + 1)
                nc.scalar.activation(bbuf[:, :, 0, :], dbuf[:, s], ACT.Exp).then_inc(a_exp[s], 1)
                if not first:
                    act.wait_ge(a_sc[s], j * (16 * G))
                nc.scalar.activation(st[:, s, :, 2 * DD:TW], amax[:, s], ACT.Copy).then_inc(a_max[s], 1)

            for s in range(2):
                products(0, s, True)
            for s in range(2):
                weights(0, s, True)
                products(1, s, False)
            with act.Fori(1, AHALF - 1) as j:
                for s in range(2):
                    weights(j, s, False)
                    products(j + 1, s, False)
            for s in range(2):
                weights(AHALF - 1, s, False)
            asked(ab[:], ab[:], ACT.Exp)
            asked(bbuf[:, 0], bbuf[:, 0], ACT.Exp)
            for c in range(NCH):
                acted[0] += 1
                act.wait_ge(s_asked, acted[0])
                nc.scalar.activation(dbuf[:, c % 2, 0:DC, :], nodes[c % len(nodes)][:, :, 0, :], ACT.Ln).then_inc(s_ln, 1)
                act.wait_ge(s_ln, c + 1)
                nc.scalar.activation(dbuf[:, c % 2, 0:DC, :], dbuf[:, c % 2, 0:DC, :], ACT.Exp, scale=-1.0).then_inc(s_acted, 1)
            asked(st3[:], st2[:], ACT.Sqrt)
            dense(0)
            asked(st3[:], st2[:], ACT.Sqrt)
            for i in range(1, 5):
                dense(i)
            asked(nu[:], nt[:], ACT.Exp)
            asked(st2[:], st1[:], ACT.Ln)
            asked(st3[:], st2[:], ACT.Sqrt)

        @block.tensor
        def _(pe):
            def carry(i, tail):
                pe.wait_ge(s_tail, 1 + i)
                m = tail.shape[1]
                for c in range(-(-m // P)):
                    w = min(P, m - c * P)
                    last = nc.tensor.transpose(ps[0:w, c // PB, (c % PB) * P:(c % PB + 1) * P], tail[:, c * P:c * P + w], idm[:])
                last.then_inc(s_turn, 1)
                pe.wait_ge(s_car, 1 + i)
                for c in range(-(-m // P)):
                    w = min(P, m - c * P)
                    source = cT[:, c, :] if m > P else carryT[:]
                    last = nc.tensor.transpose(ps[:, 2 + c // PB, (c % PB) * P:(c % PB) * P + w], source, idm[0:w, 0:w])
                last.then_inc(s_back, 1)

            def dense(i, w, v):
                pe.wait_ge(s_din, i + 1)
                for c in range(NCH):
                    last = nc.tensor.transpose(ps[0:DW, c // PB, (c % PB) * P:(c % PB + 1) * P],
                                               v[:, c * DC:(c + 1) * DC, :].rearrange("p b c -> p (b c)"), idm[:])
                last.then_inc(s_dtr, 1)
                pe.wait_ge(s_dcp, i + 1)
                for c in range(NCH):
                    last = nc.tensor.matmul(ps[:, 2 + c // PB, (c % PB) * DW:(c % PB + 1) * DW], vT[0:DW, c, :], bd[0:DW, w, :],
                                            start=True, stop=True)
                last.then_inc(s_dmm, 1)

            def narrow_pass(n):
                q, done = narrow, n * HALF
                pe.wait_ge(s_parts, n + 1)

                def fetch(j, s, first):
                    pe.wait_ge(q["hot"][s], done + j + 1)
                    if not first:
                        pe.wait_ge(q["read"][s], done + j)
                    for t in range(R):
                        for m in range(Q):
                            for part in range(3):
                                last = nc.tensor.matmul(
                                    ps[:, 4 * s + t // PB, (t % PB) * QW:(t % PB + 1) * QW].rearrange("p (q c) -> p q c", c=D),
                                    hot[s][:, m, t * P:(t + 1) * P], parts[:, m * Q:(m + 1) * Q, part, :],
                                    start=m == 0 and part == 0, stop=m == Q - 1 and part == 2)
                    last.then_inc(q["pick"][s], 1)

                if n == 0:
                    for s in range(2):
                        fetch(0, s, True)
                with pe.Fori(1 if n == 0 else 0, HALF) as j:
                    for s in range(2):
                        fetch(j, s, False)

            pe.wait_ge(s_const, 16 * 9)
            pe.wait_ge(s_zero, 4)
            pe.wait_ge(s_part, 1)
            nc.tensor.matmul(ps[:, 5, 0:1], ones[:], fcol[:, 4:5], start=True, stop=True).then_inc(s_total, 1)
            pe.wait_ge(s_flag, 1)
            unsorted = pe.value_load(flag[0:1, 0:1], min_val=0, max_val=P * K)
            with pe.If(unsorted > 0):
                with pe.Fori(0, K) as k:
                    pe.wait_ge(q_diag, k + 1)
                    nc.tensor.matmul(ps[:, 5, 0:P], ones[:], diag[:, 0, :], start=True, stop=True).then_inc(q_all, 1)
            pe.end_ifs()
            pe.wait_ge(s_quot, 1)
            for c in range(K // DW):
                last = nc.tensor.transpose(ps[0:DW, c // PB, (c % PB) * P:(c % PB + 1) * P], quotf[:, c * DW:(c + 1) * DW], idm[:])
            last.then_inc(s_quot, 1)
            pe.wait_ge(s_diag, 1)
            nc.tensor.matmul(ps[:, 4, 0:3 * P], ones[:], diag[:].rearrange("p a q -> p (a q)"), start=True, stop=True).then_inc(s_rows, 1)
            tail = run[:, 1, U - 1, :]
            narrow_pass(0)
            carry(0, tail)

            pe.wait_ge(s_w, 16 * (5 * DC + D))

            def turn(j, s, k):
                for c in range(3):
                    last = nc.tensor.transpose(ps[0:CW, G, c * P:(c + 1) * P], z[:, s, k, FROM[c] * F:FROM[c] * F + CW], idm[:])
                last.then_inc(a_tr[s], 1)

            def group(j, s, old):
                pe.wait_ge(a_z[s], j + 1)
                if old:
                    pe.wait_ge(a_trs[1 - s], (j + s) * G)
                turn(j, s, 0)
                for k in range(G):
                    pe.wait_ge(a_trs[s], j * G + k + 1)
                    if k + 1 < G:
                        turn(j, s, k + 1)
                    if old and k in (0, HG):
                        pe.wait_ge(a_out[1 - s], (j + s) * 2 - (1 if k == 0 else 0))
                    for c in range(3):
                        w = (NEW[c + 1] - NEW[c]) * 2 * D
                        last = nc.tensor.matmul(ps[:, k, NEW[c] * 2 * D:NEW[c] * 2 * D + w],
                                                zT[0:CW, (s * G + k) % 2, c * P:(c + 1) * P], wsb[0:CW, c, 0:w], start=True, stop=True)
                    if k in (HG - 1, G - 1):
                        last.then_inc(a_mm[s], 1)

            pe.wait_ge(s_feat, 1)
            group(0, 0, False)
            group(0, 1, True)
            with pe.Fori(1, AHALF) as j:
                for s in range(2):
                    group(j, s, True)
            carry(1, st[:, 1, G - 1, :])
            narrow_pass(1)
            carry(2, tail)
            dense(0, 0, nt)
            narrow_pass(2)
            carry(3, tail)
            dense(1, 1, nt)
            dense(2, 2, nt)
            narrow_pass(3)
            carry(4, tail)
            dense(3, 3, nt)
            dense(4, 4, nt)

        @block.vector
        def _(dve):
            v = nc.vector
            chained = [0]
            looped = [0]

            def link(ins):
                chained[0] += 1
                ins.then_inc(s_chain, 1)
                dve.wait_ge(s_chain, chained[0])

            def loop_start():
                looped[0] = 0
                dve.sem_clear(s_loop)

            def hold(ins):
                looped[0] += 1
                ins.then_inc(s_loop, 1)
                dve.wait_ge(s_loop, looped[0])

            def wide(ap):
                return ap.unsqueeze(2).to_broadcast([P, ap.shape[1], D])

            def everywhere(row):
                return row.unsqueeze(1).to_broadcast([P, NB, D])

            def tt(dest, a, b, op):
                return v.tensor_tensor(dest, a, b, op)

            asks = [0]

            def ask(ins):
                asks[0] += 1
                ins.then_inc(s_asked, 1)
                dve.wait_ge(s_acted, asks[0])

            def split(features):
                link(v.tensor_copy(parts[:, :, 0, :], features[:]))
                link(tt(nt[:], features[:], parts[:, :, 0, :], ALU.subtract))
                link(v.tensor_copy(parts[:, :, 1, :], nt[:]))
                link(tt(nt[:], nt[:], parts[:, :, 1, :], ALU.subtract))
                v.tensor_copy(parts[:, :, 2, :], nt[:]).then_inc(s_parts, 1)

            def dst_list(after):
                after(v.tensor_copy(dstf[:, 1:K + 1], dsti))
                after(v.tensor_copy(edgef[:], edgei[:]))
                after(v.tensor_copy(dstf[:, 0:1], edgef[:, 0:1]))
                after(v.tensor_copy(dstf[:, K + 1:K + 2], edgef[:, 2:3]))

            def sort():
                def q_start():
                    dve.sem_clear(q_chain)
                    sorted_[0] = 0

                def after(ins):
                    sorted_[0] += 1
                    ins.then_inc(q_chain, 1)
                    dve.wait_ge(q_chain, sorted_[0])

                sorted_ = [0]
                q_start()
                dve.wait_ge(q_place, 1)
                after(v.tensor_copy(lower[:], loweri[:]))
                after(v.tensor_scalar(lower[:], lower[:], 0.0, None, ALU.is_lt))
                after(v.memset(place[:], 0.0))
                with dve.Fori(0, P) as r:
                    q_start()
                    dve.wait_ge(q_row, r * 16 + 16)
                    for b in range(NB):
                        after(v.tensor_scalar(junk, srci, nid[:, b:b + 1], 0.0, ALU.is_lt, ALU.add, accum_out=below[:, b:b + 1]))
                    tt(place[:], place[:], below[:], ALU.add).then_inc(q_rowu, 1)
                    dve.wait_ge(q_rowu, r + 1)
                dve.wait_ge(q_rowu, P)
                v.memset(tcol[:], 0.0).then_inc(q_place, 1)
                with dve.Fori(0, K) as k:
                    q_start()
                    dve.wait_ge(q_load, k + 1)
                    node, rank, equals, new, last = (tcol[:, c:c + 1] for c in range(5))
                    after(v.tensor_copy(node, key[:, 0:1]))
                    v.tensor_scalar(diag[:, 0, :], idm[:], node, None, ALU.mult).then_inc(q_diag, 1)
                    dve.wait_ge(q_all, k + 1)
                    after(v.tensor_scalar(diag[:, 1, :], ps[:, 5, 0:P], node, 0.0, ALU.is_equal, ALU.add, accum_out=equals))
                    after(tt(diag[:, 2, :], diag[:, 1, :], lower[:], ALU.mult))
                    after(v.tensor_reduce(rank, diag[:, 2, :], AX.X, ALU.add))
                    dve.wait_ge(q_got, k * 16 + 16)
                    after(tt(new, got_place[:], rank, ALU.add))
                    after(v.tensor_copy(spot[:, 0:1], new))
                    after(v.tensor_scalar(spot[:, 1:2], new, float(K), None, ALU.add))
                    after(tt(new, got_place[:], equals, ALU.add))
                    after(tt(last, equals, rank, ALU.subtract))
                    after(v.tensor_scalar(last, last, 1.5, OOB, ALU.is_gt, ALU.mult))
                    tt(spot[:, 2:3], last, node, ALU.add).then_inc(q_spot, 1)
                    dve.wait_ge(q_spot, k + 1)
                q_start()
                dve.wait_ge(q_again, 16 * 5)
                dst_list(after)

            dve.wait_ge(s_list, 16 * 5)
            dve.wait_ge(s_iota, 4)
            link(v.tensor_copy(nid[:], nidi[:]))
            dst_list(link)
            link(tt(junk, dstf[:, 1:K + 1], dstf[:, 2:K + 2], ALU.is_gt))
            v.tensor_reduce(fcol[:, 4:5], junk, AX.X, ALU.add).then_inc(s_part, 1)
            dve.wait_ge(s_total, 1)
            v.tensor_copy(flag[:], ps[:, 5, 0:1]).then_inc(s_flag, 1)
            dve.wait_ge(s_const, 16 * 9)
            dve.wait_ge(s_flag, 1)
            unsorted = dve.value_load(flag[0:1, 0:1], min_val=0, max_val=P * K)
            with dve.If(unsorted > 0):
                sort()
            dve.end_ifs()
            link(v.tensor_copy(count[:], counti[:]))
            srcf, trial = quot_src, junk
            link(v.tensor_copy(srcf, srci))
            link(v.tensor_scalar(srci, srcf, 1.0 / Q, None, ALU.mult))
            link(v.tensor_copy(quotf, srci))
            link(v.scalar_tensor_tensor(trial, quotf, -float(Q), srcf, ALU.mult, ALU.add))
            over = scat[:]
            link(v.tensor_scalar(over, trial, Q - 0.5, None, ALU.is_gt))
            link(tt(quotf, quotf, over, ALU.add))
            link(v.tensor_scalar(over, trial, 0.0, None, ALU.is_lt))
            link(tt(quotf, quotf, over, ALU.subtract))
            v.scalar_tensor_tensor(rem[:], quotf, -float(Q), srcf, ALU.mult, ALU.add).then_inc(s_quot, 1)
            dve.wait_ge(s_quot, 2)
            for b in range(4):
                chunks = min(PB, K // DW - b * PB)
                last = v.tensor_copy(quotT[0:DW, b * PB:b * PB + chunks, :],
                                     ps[0:DW, b, 0:chunks * P].rearrange("p (c q) -> p c q", q=P))
            last.then_inc(s_quot, 1)
            first = dstf[:, 1:2]
            link(tt(fcol[:, 0:1], first, dstf[:, 0:1], ALU.is_equal))
            link(tt(fcol[:, 1:2], edgef[:, 0:1], edgef[:, 1:2], ALU.is_equal))
            link(tt(fcol[:, 1:2], fcol[:, 0:1], fcol[:, 1:2], ALU.mult))
            link(v.tensor_scalar(diag[:, 0, :], idm[:], first, None, ALU.mult))
            link(v.tensor_scalar(diag[:, 1, :], idm[:], fcol[:, 0:1], None, ALU.mult))
            v.tensor_scalar(diag[:, 2, :], idm[:], fcol[:, 1:2], None, ALU.mult).then_inc(s_diag, 1)
            dve.wait_ge(s_rows, 1)
            link(v.tensor_copy(frow[:], ps[:, 4, 0:P]))
            link(v.tensor_copy(rows[:, 0:2, :], ps[:, 4, P:3 * P].rearrange("p (a q) -> p a q", q=P)))
            link(v.tensor_scalar(rows[:, 2:4, :], rows[:, 0:2, :], 1.0, BIG, ALU.subtract, ALU.mult))
            link(tt(compared, frow[:].unsqueeze(1).to_broadcast([P, NG, P]),
                    nid[:, 0:NG].unsqueeze(2).to_broadcast([P, NG, P]), ALU.is_le))
            link(v.tensor_reduce(pidx[:], compared, AX.X, ALU.add))
            link(v.tensor_scalar(pidx[:], pidx[:], 1.0, None, ALU.max))

            def next_slice(g, s):
                v.tensor_copy(pring[:, s:s + 1], pidx[:, bass.ds(g, 1)]).then_inc(s_pidx[s], 1)

            for s in range(2):
                next_slice(s, s)
            split(x0)
            dve.wait_ge(s_quots, 16)
            link(tt(keep, dstf[:, 1:K + 1], dstf[:, 0:K], ALU.is_equal))
            link(v.memset(keep[:, 0:1], 0.0))
            link(v.tensor_scalar(neg, keep, 1.0, BIG, ALU.subtract, ALU.mult))
            link(tt(scat[:], dstf[:, 1:K + 1], dstf[:, 2:K + 2], ALU.is_equal))
            link(v.scalar_tensor_tensor(scat[:], scat[:], OOB, dstf[:, 1:K + 1], ALU.mult, ALU.add))
            link(v.tensor_scalar(junk, dstf[:, 1:K + 1], first, 0.0, ALU.is_equal, ALU.add, accum_out=fcol[:, 2:3]))
            link(tt(fidx[:, 0:1], fcol[:, 2:3], nid[:, NG:NG + 1], ALU.add))
            link(v.tensor_copy(fidx[:, 1:2], first))
            link(tt(fcol[:, 3:4], first, dstf[:, K + 1:K + 2], ALU.is_equal))
            link(v.tensor_scalar(fcol[:, 3:4], fcol[:, 3:4], -1.0, 1.0, ALU.mult, ALU.add))
            link(tt(fcol[:, 3:4], fcol[:, 3:4], fcol[:, 0:1], ALU.mult))
            link(v.tensor_scalar(fcol[:, 3:4], fcol[:, 3:4], -OOB, OOB, ALU.mult, ALU.add))
            link(tt(fidx[:, 2:3], fcol[:, 3:4], first, ALU.add))
            def narrow_pass(n):
                q, done = narrow, n * HALF
                most = n == 1
                mask = neg if most else keep

                def one_hots(j, s, first):
                    dve.wait_ge(q["quot"][s], 16 * (done + j + 1))
                    if not first:
                        dve.wait_ge(q["pick"][s], done + j)
                    for m in range(Q):
                        last = v.tensor_scalar(hot[s][:, m, :], quot[:, s, :], count[:, 0, m:m + 1], None, ALU.is_equal)
                    last.then_inc(q["hot"][s], 1)

                def pick(j, s):
                    hold(tt(amask[:], rem[:, bass.ds((2 * j + s) * U + A, R)].unsqueeze(2).to_broadcast([P, R, Q]),
                            count[:, 1, :].unsqueeze(1).to_broadcast([P, R, Q]), ALU.is_equal))
                    dve.wait_ge(q["pick"][s], done + j + 1)
                    for b in range(-(-R // PB)):
                        steps = min(PB, R - b * PB)
                        last = tt(picked[:, b * PB:b * PB + steps],
                                  ps[:, 4 * s + b, 0:steps * QW].rearrange("p (r q c) -> p r q c", q=Q, c=D),
                                  amask[:, b * PB:b * PB + steps].unsqueeze(3).to_broadcast([P, steps, Q, D]), ALU.mult)
                    last.then_inc(q["read"][s], 1)
                    dve.wait_ge(q["read"][s], done + j + 1)
                    hold(v.tensor_reduce(msg[:, s, A:U, :], picked.rearrange("p r q c -> p r c q"), AX.X, ALU.add))

                def round_(j, more, first):
                    loop_start()
                    for s in range(2):
                        g = 2 * j + s
                        if more or s == 0:
                            one_hots(j + s, 1 - s, first and s == 0)
                        pick(j, s)
                        hold(v.tensor_copy(mring[:, s, :], mask[:, bass.ds(g * U, U)]))
                        dve.wait_ge(q["got"][s], (done + j + 1) * (16 * A))
                        values = msg
                        if n < 2:
                            dve.wait_ge(q["w"][s], 16 * (done + j + 1))
                            tt(val[:, s], msg[:, s], wts[:, s, :].unsqueeze(2).to_broadcast([P, U, D]),
                               ALU.mult).then_inc(q["mul"][s], 1)
                            values = val
                            dve.wait_ge(q["act"][s] if n == 0 else q["mul"][s], done + j + 1)
                        if not first:
                            dve.wait_ge(q["put"][s], 16 * (done + j))
                        for c in range(D):
                            last = v.tensor_tensor_scan(run[:, s, :, c], mring[:, s, :], values[:, s, :, c], run[:, 1 - s, U - 1, c:c + 1],
                                                        ALU.add if most else ALU.mult, ALU.max if most else ALU.add)
                        last.then_inc(q["run"][s], 1)
                        dve.wait_ge(q["run"][s], done + j + 1)
                        if n == 0:
                            dve.wait_ge(s_slice[s], 16 * (j + 1))
                            node = nid[:, bass.ds(g, 1)]
                            hold(v.tensor_scalar(junk, slices[:, s, :], node, 0.0, ALU.is_le, ALU.add,
                                                 accum_out=cle[:, bass.ds(g, 1)]))
                            hold(v.tensor_scalar(junk, slices[:, s, :], node, 0.0, ALU.is_lt, ALU.add,
                                                 accum_out=clt[:, bass.ds(g, 1)]))
                            if more:
                                next_slice(g + 2, s)

                link(v.memset(run[:, 1, U - 1, :], 0.0))
                one_hots(0, 0, n == 0)
                if n == 0:
                    round_(0, True, True)
                with dve.Fori(1 if n == 0 else 0, HALF - 1) as j:
                    round_(j, True, False)
                round_(HALF - 1, False, False)
                if n == 0:
                    link(v.tensor_scalar(endf[:], pidx[:, 0:NB], -1.0, float(K), ALU.add, ALU.mult))
                    link(tt(endf[:], endf[:], cle[:, 0:NB], ALU.add))
                    link(v.tensor_scalar(endf[:], endf[:], -1.0, 0.0, ALU.add, ALU.max))
                    link(tt(full[:], clt[:, 0:NB], cle[:, 0:NB], ALU.is_lt))
                    link(v.tensor_scalar(st1[:], nid[:, 0:NB], float(N), None, ALU.is_ge))
                    link(tt(full[:], full[:], st1[:], ALU.max))
                    v.tensor_copy(endi[:], endf[:]).then_inc(s_idxr, 1)
                i = 0 if n == 0 else n + 1
                v.memset(tailT[:, 0:1], -BIG if most else 0.0).then_inc(s_tail, 1)
                dve.wait_ge(s_turn, i + 1)
                link(tt(tailT[:, 1:P], ps[0:D, 0, 0:P - 1], rows[0:D, CONT_NEG if most else CONT, 1:P], ALU.add if most else ALU.mult))
                v.tensor_tensor_scan(carryT[:], rows[0:D, BOTH_NEG if most else BOTH, :], tailT[:], 0.0,
                                     ALU.add if most else ALU.mult, ALU.max if most else ALU.add).then_inc(s_car, 1)
                dve.wait_ge(s_back, i + 1)
                dve.wait_ge(s_fixed, 16 * (2 * i + 1))
                tt(lead2[:], lead[:], ps[:, 2, 0:D], ALU.max if most else ALU.add).then_inc(s_lead, 1)
                dve.wait_ge(s_node[n], 16 * NB)

            def layer_norm(dest, source):
                link(v.tensor_reduce(st1[:], source[:], AX.X, ALU.add))
                link(v.tensor_scalar(st1[:], st1[:], 1.0 / D, None, ALU.mult))
                link(tt(nt[:], source[:], wide(st1[:]), ALU.subtract))
                link(tt(nu[:], nt[:], nt[:], ALU.mult))
                link(v.tensor_reduce(st2[:], nu[:], AX.X, ALU.add))
                ask(v.tensor_scalar(st2[:], st2[:], 1.0 / D, EPS, ALU.mult, ALU.add))
                link(v.reciprocal(st3[:], st3[:]))
                return tt(dest[:], nt[:], wide(st3[:]), ALU.mult)

            def attention():
                link(v.memset(amax[:, 1, G - 1, :], 0.0))
                link(v.memset(st[:, 1, G - 1, 0:2 * DD], 0.0))

                def mark(ins):
                    looped[0] += 1
                    ins.then_inc(s_loop, 1)
                    return looped[0]

                def need(count):
                    dve.wait_ge(s_loop, count)

                def outer(j, s, first=False):
                    dve.wait_ge(a_ef[s], 16 * (j + 1))
                    dve.wait_ge(a_got[s], (j + 1) * (16 * G))
                    if not first:
                        dve.wait_ge(a_tr[s], j * G)
                    tt(z[:, s].rearrange("p g (i f) -> p g i f", f=F),
                       efs[:, s].rearrange("p (g f) -> p g f", f=F).unsqueeze(2).to_broadcast([P, G, D, F]),
                       hsrc[:, s].unsqueeze(3).to_broadcast([P, G, D, F]), ALU.mult).then_inc(a_z[s], 1)

                def ring_copy(j, s):
                    return v.tensor_copy(aring[:, s], resets[:, :, bass.ds((2 * j + s) * G, G)])

                def running_max(j, s, k):
                    if k == 0:
                        dve.wait_ge(a_out[s], j * 2 + 1)
                    if k == HG:
                        dve.wait_ge(a_out[s], j * 2 + 2)
                    return mark(v.scalar_tensor_tensor(amax[:, s, k, :], amax[:, 1 - s, G - 1, :] if k == 0 else amax[:, s, k - 1, :],
                                                       aring[:, s, 0, k:k + 1], dbuf[:, s, k, :], ALU.add, ALU.max))

                def segment_max(s, k):
                    return mark(v.scalar_tensor_tensor(smax[:, k, :], amax[:, s, G - 1, :] if k == G - 2 else smax[:, k + 1, :],
                                                       aring[:, s, 0, k + 1:k + 2], amax[:, s, k, :], ALU.add, ALU.max))

                def last_difference(s):
                    tt(dbuf[:, s, G - 1, :], dbuf[:, s, G - 1, :], amax[:, s, G - 1, :], ALU.subtract)

                def differences(s, last):
                    need(last)
                    tt(dbuf[:, s, 0:G - 1, :], dbuf[:, s, 0:G - 1, :], smax[:], ALU.subtract)
                    v.scalar_tensor_tensor(dbuf[:, s, G, :], amax[:, 1 - s, G - 1, :], aring[:, s, 0, 0:1], smax[:, 0, :],
                                           ALU.add, ALU.subtract).then_inc(a_d[s], 1)

                def weighted(j, s):
                    dve.wait_ge(a_exp[s], j + 1)
                    tt(bbuf[:, 0:G, 1, :], mbuf[:, s], bbuf[:, 0:G, 0, :], ALU.mult).then_inc(a_w[s], 1)

                def rescaled(s):
                    return mark(tt(stt[:], st[:, 1 - s, G - 1, 0:2 * DD].rearrange("p (t c) -> p t c", t=2),
                                   bbuf[:, G, 0, :].unsqueeze(1).to_broadcast([P, 2, DD]), ALU.mult))

                def store_index(j, s, first):
                    if not first:
                        dve.wait_ge(a_sc[s], j * (16 * G))
                    v.tensor_copy(scidx[:, s, :], scat[:, bass.ds((2 * j + s) * G, G)])

                def running_sum(s, k):
                    if k == 0:
                        return tt(st[:, s, 0, 0:2 * DD].rearrange("p (t c) -> p t c", t=2), stt[:], bbuf[:, 0, :, :], ALU.add)
                    return v.scalar_tensor_tensor(st[:, s, k, 0:2 * DD], st[:, s, k - 1, 0:2 * DD], aring[:, s, 1, k:k + 1],
                                                  bbuf[:, k, :, :].rearrange("p t c -> p (t c)"), ALU.mult, ALU.add)

                def maxima_turn(j, s, i):
                    return running_max(j, s, i) if i < G else segment_max(s, 2 * G - 2 - i)

                def step(j, s, first, last, ahead):
                    b, jb = 1 - s, j - 1 + s
                    if ahead:
                        outer(jb + 1, b)
                    if not first:
                        dve.wait_ge(a_max[s], j)
                    m = running_max(j, s, 0)
                    weighted(jb, b)
                    need(m)
                    m = running_max(j, s, 1)
                    t = rescaled(b)
                    for k in range(G - 1):
                        need(m)
                        m = maxima_turn(j, s, k + 2)
                        need(t)
                        t = mark(running_sum(b, k))
                    need(m)
                    m = maxima_turn(j, s, G + 1)
                    dve.wait_ge(a_max[b], jb + 1)
                    need(t)
                    running_sum(b, G - 1).then_inc(a_st[b], 1)
                    need(m)
                    m = maxima_turn(j, s, G + 2)
                    last_difference(s)
                    for i in range(G + 3, 2 * G - 1):
                        need(m)
                        m = maxima_turn(j, s, i)
                        if i == G + 3 and not last:
                            ring_copy(jb + 1, b)
                        if i == G + 4:
                            store_index(j, s, first)
                    differences(s, m)
                    dve.wait_ge(a_st[b], jb + 1)

                for s in range(2):
                    outer(0, s, True)
                loop_start()
                ring_copy(0, 0)
                need(mark(ring_copy(0, 1)))
                for i in range(2 * G - 1):
                    last = maxima_turn(0, 0, i)
                    need(last)
                last_difference(0)
                store_index(0, 0, True)
                differences(0, last)
                step(0, 1, True, False, True)
                step(1, 0, False, False, True)
                with dve.Fori(1, AHALF - 1) as j:
                    loop_start()
                    step(j, 1, False, False, True)
                    step(j + 1, 0, False, False, True)
                loop_start()
                step(AHALF - 1, 1, False, True, False)
                loop_start()
                weighted(AHALF - 1, 1)
                need(rescaled(1))
                dve.wait_ge(a_max[1], AHALF)
                for k in range(G - 1):
                    need(mark(running_sum(1, k)))
                running_sum(1, G - 1).then_inc(a_st[1], 1)
                dve.wait_ge(a_st[1], AHALF)

                for half in range(2):
                    link(v.memset(tT[:, 4 + half, 0:1], -BIG))
                v.memset(tT[:, 0:4, 0:1], 0.0).then_inc(s_tail, 1)
                dve.wait_ge(s_turn, 2)
                link(v.tensor_copy(tT[:, 0:4, 1:P], ps[:, 0, :].rearrange("p (c q) -> p c q", q=P)[:, :, 0:P - 1]))
                for half in range(2):
                    m, c = tT[:, 4 + half, :], cT[:, 4 + half, :]
                    link(tt(m[:, 1:P], ps[:, 1, half * P:half * P + P - 1], rows[:, CONT_NEG, 1:P], ALU.add))
                    link(v.tensor_tensor_scan(c, rows[:, BOTH_NEG, :], m, 0.0, ALU.add, ALU.max))
                    link(v.memset(ab[:, half, 0, 0:1], 0.0))
                    link(tt(ab[:, half, 0, 1:P], rows[:, BOTH_NEG, 1:P], c[:, 0:P - 1], ALU.add))
                    link(tt(ab[:, half, 0, 1:P], ab[:, half, 0, 1:P], c[:, 1:P], ALU.subtract))
                    last = tt(ab[:, half, 1, :], m, c, ALU.subtract)
                    if half == 0:
                        link(last)
                ask(last)
                for t in range(4):
                    link(tt(tT[:, t, :], tT[:, t, :], ab[:, t % 2, 1, :], ALU.mult))
                    last = v.tensor_tensor_scan(cT[:, t, :], ab[:, t % 2, 0, :], tT[:, t, :], 0.0, ALU.mult, ALU.add)
                last.then_inc(s_car, 1)
                dve.wait_ge(s_back, 2)
                dve.wait_ge(s_fixed, 16 * 3)
                mine, done, w = st[:, 0, 0, :], st[:, 0, 1, :], bbuf[:, 0]
                theirs = stt[:].rearrange("p t c -> p (t c)")
                link(tt(done[:, 2 * DD:TW], mine[:, 2 * DD:TW], ps[:, 3, 0:DD], ALU.max))
                link(tt(w[:, 0, :], mine[:, 2 * DD:TW], done[:, 2 * DD:TW], ALU.subtract))
                ask(tt(w[:, 1, :], ps[:, 3, 0:DD], done[:, 2 * DD:TW], ALU.subtract))
                for t in range(2):
                    part = slice(t * DD, (t + 1) * DD)
                    link(tt(theirs[:, part], ps[:, 2, part], w[:, 1, :], ALU.mult))
                    link(tt(done[:, part], mine[:, part], w[:, 0, :], ALU.mult))
                link(tt(done[:, 0:2 * DD], done[:, 0:2 * DD], theirs, ALU.add))
                link(v.memset(nt[:, 0:1, :], 0.0))
                v.memset(nt[:, 0:1, :], 0.0).then_inc(s_lead, 1)

                def sums(c):
                    dve.wait_ge(s_att[c], 16)
                    b = nodes[c % len(nodes)][:, :, 0, :]
                    v.tensor_scalar(b, b, TINY, None, ALU.max).then_inc(s_asked, 1)

                sums(0)
                for c in range(NCH):
                    if c + 1 < NCH:
                        sums(c + 1)
                    asks[0] += 1
                    dve.wait_ge(s_acted, asks[0])
                    total, weighted_sum = (nodes[c % len(nodes)][:, :, t, :] for t in range(2))
                    r = dbuf[:, c % 2, 0:DC, :]
                    link(tt(total, total, r, ALU.mult))
                    link(v.tensor_scalar(total, total, -1.0, 2.0, ALU.mult, ALU.add))
                    link(tt(weighted_sum, weighted_sum, r, ALU.mult))
                    link(tt(total, weighted_sum, total, ALU.mult))
                    v.tensor_reduce(got[:, c * DC:(c + 1) * DC, :], total.rearrange("p b (i o) -> p b o i", o=D),
                                    AX.X, ALU.add).then_inc(s_attu, 1)
                dve.wait_ge(s_attu, NCH)

            products = [0]

            def dense(dest, ins, b, relu):
                ins.then_inc(s_din, 1)
                products[0] += 1
                dve.wait_ge(s_dmm, products[0])
                for half, (lo, hi) in enumerate(((0, PB * DC), (PB * DC, NB))):
                    link(tt(dest[:, lo:hi, :], ps[:, 2 + half, 0:(hi - lo) * D].rearrange("p (b c) -> p b c", c=D),
                            bias[:, b, :].unsqueeze(1).to_broadcast([P, hi - lo, D]), ALU.add))
                if relu:
                    link(v.tensor_scalar(dest[:], dest[:], 0.0, None, ALU.max))

            narrow_pass(0)
            link(tt(got[:], got[:], wide(full[:]), ALU.mult))
            link(tt(got[:], got[:], x0[:], ALU.add))
            layer_norm(xa, got).then_inc(s_feat, 1)
            attention()
            link(tt(got[:], got[:], xa[:], ALU.add))
            layer_norm(xb, got).then_inc(s_feat, 1)
            dve.wait_ge(s_feat, 2)
            split(xb)
            narrow_pass(1)
            dense(got, tt(nt[:], got[:], wide(full[:]), ALU.mult), 0, False)
            link(tt(got[:], got[:], xb[:], ALU.add))
            link(layer_norm(xa, got))
            link(v.tensor_scalar(bad[:], full[:], -POISON, POISON, ALU.mult, ALU.add))
            link(tt(xa[:], xa[:], wide(full[:]), ALU.mult))
            tt(xa[:], xa[:], wide(bad[:]), ALU.add).then_inc(s_feat, 1)
            dve.wait_ge(s_feat, 3)
            split(xa)
            for i, (own, dest) in enumerate(((xa, xb), (xb, got))):
                narrow_pass(2 + i)
                link(tt(nu[:], got[:], wide(full[:]), ALU.mult))
                link(tt(nt[:], nu[:], own[:], ALU.add))
                link(v.tensor_scalar(bad[:], nt[:, :, 0], POISON * 0.5, None, ALU.is_gt))
                link(v.tensor_scalar(st1[:], bad[:], -1.0, 1.0, ALU.mult, ALU.add))
                link(v.scalar_tensor_tensor(nt[:], own[:], epsb[:, i:i + 1], nt[:], ALU.mult, ALU.add))
                dense(got, tt(nt[:], nt[:], wide(st1[:]), ALU.mult), 1 + 2 * i, True)
                dense(dest, v.tensor_copy(nt[:], got[:]), 2 + 2 * i, i == 0)
                if i == 0:
                    link(tt(dest[:], dest[:], wide(st1[:]), ALU.mult))
                    link(v.tensor_scalar(st2[:], bad[:], POISON, None, ALU.mult))
                    tt(dest[:], dest[:], wide(st2[:]), ALU.add).then_inc(s_feat, 1)
                    dve.wait_ge(s_feat, 4)
                    split(xb)
            link(v.tensor_reduce(st1[:], got[:], AX.X, ALU.max))
            ask(tt(nt[:], got[:], wide(st1[:]), ALU.subtract))
            ask(v.tensor_reduce(st1[:], nu[:], AX.X, ALU.add))
            link(tt(nt[:], nt[:], wide(st2[:]), ALU.subtract))
            link(v.tensor_scalar(st1[:], bad[:], -1.0, 1.0, ALU.mult, ALU.add))
            link(tt(xa[:], xa[:], wide(st1[:]), ALU.mult))
            link(tt(got[:], nt[:], xa[:], ALU.add))
            link(layer_norm(got, got))
            link(v.tensor_scalar(bad[:], bad[:], BIG, BIG, ALU.mult, ALU.mult))
            link(tt(bad[:], bad[:], bad[:], ALU.subtract))
            tt(nt[:], got[:], wide(bad[:]), ALU.add).then_inc(s_feat, 1)


def kernel(x, src, dst, edge_attr_16, edge_weight, edge_weight1, L1_gnn_W_msg, L1_gnn_b_msg, L1_gnn_W_attn,
           L1_gnn_b_attn, L2_gnn_W, L2_gnn_b, L3_gnn_eps1, L3_gnn_w1a, L3_gnn_b1a, L3_gnn_w1b, L3_gnn_b1b,
           L3_gnn_eps2, L3_gnn_w2a, L3_gnn_b2a, L3_gnn_w2b, L3_gnn_b2b):
    import numpy as np
    import concourse.bacc as bacc
    from concourse.bass_utils import run_bass_kernel_spmd as run

    def padded(a, rows, fill=0):
        a = np.asarray(a)
        return np.concatenate([a, np.full((rows - a.shape[0],) + a.shape[1:], fill, a.dtype)])

    d = np.asarray(dst)
    arrays = {
        "x": padded(x, NN),
        "src": padded(src, P * K).reshape(P, K),
        "dst": np.concatenate([np.full((1, K), -1, d.dtype), padded(d, P * K, N).reshape(P, K), np.full((1, K), N + 1, d.dtype)]),
        "ew": padded(edge_weight, P * K).reshape(P, K),
        "ew1": padded(edge_weight1, P * K).reshape(P, K),
        "ef": np.concatenate([padded(edge_attr_16, P * K), np.ones((P * K, 1), np.float32)], 1).reshape(P, K * F),
        "att_w": np.stack([np.concatenate([np.asarray(w), np.asarray(b)[None]]).reshape(F, D, D) for w, b in (
            (L1_gnn_W_attn, L1_gnn_b_attn), (L1_gnn_W_msg, L1_gnn_b_msg))], 2).reshape(F, 2 * DD),
        "ident": np.eye(P, dtype=np.float32),
        "dense_w": np.stack([np.asarray(L2_gnn_W).T] + [np.asarray(w) for w in (L3_gnn_w1a, L3_gnn_w1b, L3_gnn_w2a, L3_gnn_w2b)]),
        "biases": np.stack([np.asarray(b) for b in (L2_gnn_b, L3_gnn_b1a, L3_gnn_b1b, L3_gnn_b2a, L3_gnn_b2b)]),
        "eps": np.stack([np.asarray(L3_gnn_eps1), np.asarray(L3_gnn_eps2)]),
    }
    arrays = {k: np.ascontiguousarray(v) for k, v in arrays.items()}
    nc = bacc.Bacc("TRN2", target_bir_lowering=False, num_devices=1)
    args = [nc.dram_tensor(f"in_{k}", v.shape, mybir.dt.from_np(v.dtype), kind="ExternalInput").ap() for k, v in arrays.items()]
    out = nc.dram_tensor("out", (NN, D), FP, kind="ExternalOutput").ap()
    gnn_program(nc, *args, out)
    result = run(nc, [{f"in_{k}": v for k, v in arrays.items()}], core_ids=[0])
    return result.results[0]["out"][:N]
```
